# Optimizing a Trainium2 kernel written in Bass

```python
import numpy as np
import jax
import jax.numpy as jnp

def _softmax(x, axis=-1):
    return jax.nn.softmax(x, axis=axis)

def _gelu(x):
    return jax.nn.gelu(x, approximate=True)

def _silu(x):
    return jax.nn.silu(x)

def _sigmoid(x):
    return jax.nn.sigmoid(x)

def _layernorm(x, axis=-1, eps=1e-05):
    m = jnp.mean(x, axis=axis, keepdims=True)
    v = jnp.var(x, axis=axis, keepdims=True)
    return (x - m) / jnp.sqrt(v + eps)

def _scatter_add(tgt, idx, src, axis=0):
    return tgt.at[idx].add(src)

def _segment_sum(src, seg, n):
    return jax.ops.segment_sum(src, seg, n)
kernel_name = 'mk_seq_postln_d1_jaxref_r4_f234b4'

def setup_inputs(seed: int=0):
    np.random.seed(seed)
    _w = jnp.asarray

    def _L0_attn_setup():
        import jax, jax.numpy as jnp
        import numpy as np
        from jax import lax
        B, L, DM = (1, 512, 256)
        N = 16
        K = 4
        DI = 2 * DM

        def silu(v):
            return v * jax.nn.sigmoid(v)
        key = jax.random.key(seed)
        ks = jax.random.split(key, 11)
        s = 0.02
        f32 = jnp.float32
        return {'x': jax.random.normal(ks[0], (B, L, DM), f32), 'W_in': jax.random.normal(ks[1], (2 * DI, DM), f32) * s, 'b_in': jnp.zeros((2 * DI,), f32), 'W_conv': jax.random.normal(ks[2], (DI, 1, K), f32) * s, 'b_conv': jnp.zeros((DI,), f32), 'W_x': jax.random.normal(ks[3], (DI + 2 * N, DI), f32) * s, 'b_x': jnp.zeros((DI + 2 * N,), f32), 'W_out': jax.random.normal(ks[4], (DM, DI), f32) * s, 'b_out': jnp.zeros((DM,), f32), 'A_log': jax.random.normal(ks[5], (DI, N), f32), 'D': jnp.ones((DI,), f32)}
    _L0_attn_in = _L0_attn_setup()

    def _L0_ffn_setup():
        import jax, jax.numpy as jnp
        import numpy as np
        B, S, DIM = (4, 1024, 256)
        BASE_COUPLING = 0.1
        NUM_CYCLES = 3

        def _gelu(x):
            return jax.nn.gelu(x, approximate=False)

        def _coupling_net(h, w1, b1, w2, b2, w3, b3, w4, b4):
            h = _gelu(h @ w1 + b1)
            h = _gelu(h @ w2 + b2)
            h = _gelu(h @ w3 + b3)
            return jax.nn.sigmoid(h @ w4 + b4)

        def _global_net(h, w1, b1, w2, b2, w3, b3):
            h = _gelu(h @ w1 + b1)
            h = _gelu(h @ w2 + b2)
            return jax.nn.sigmoid(h @ w3 + b3)

        def _twist(x):
            o_r, o_i, p_r, p_i = jnp.split(x, 4, axis=-1)
            return jnp.concatenate([p_r, -p_i, -o_r, o_i], axis=-1)
        key = jax.random.key(seed)
        ks = jax.random.split(key, 9)
        d = DIM

        def w(k, fan_in, fan_out):
            return jax.random.normal(k, (fan_in, fan_out), dtype=jnp.float32) / np.sqrt(fan_in).astype(np.float32)
        inp = {'x': jax.random.normal(ks[0], (B, S, d), dtype=jnp.float32)}
        cn_dims = [(d, d), (d, d // 2), (d // 2, d // 4), (d // 4, 1)]
        for i, (a, b) in enumerate(cn_dims):
            inp[f'cn_w{i + 1}'] = w(ks[1 + i], a, b)
            inp[f'cn_b{i + 1}'] = jnp.zeros((b,), dtype=jnp.float32)
        gc_dims = [(d, d // 2), (d // 2, d // 4), (d // 4, 1)]
        for i, (a, b) in enumerate(gc_dims):
            inp[f'gc_w{i + 1}'] = w(ks[5 + i], a, b)
            inp[f'gc_b{i + 1}'] = jnp.zeros((b,), dtype=jnp.float32)
        inp['adaptive_range'] = jnp.full((1,), 0.2, dtype=jnp.float32)
        return inp
    _L0_ffn_in = _L0_ffn_setup()
    _d = {'L0_attn_x': _L0_attn_in['x'], 'L0_attn_W_in': _L0_attn_in['W_in'], 'L0_attn_b_in': _L0_attn_in['b_in'], 'L0_attn_W_conv': _L0_attn_in['W_conv'], 'L0_attn_b_conv': _L0_attn_in['b_conv'], 'L0_attn_W_x': _L0_attn_in['W_x'], 'L0_attn_b_x': _L0_attn_in['b_x'], 'L0_attn_W_out': _L0_attn_in['W_out'], 'L0_attn_b_out': _L0_attn_in['b_out'], 'L0_attn_A_log': _L0_attn_in['A_log'], 'L0_attn_D': _L0_attn_in['D'], 'L0_ffn_cn_w1': _L0_ffn_in['cn_w1'], 'L0_ffn_cn_b1': _L0_ffn_in['cn_b1'], 'L0_ffn_cn_w2': _L0_ffn_in['cn_w2'], 'L0_ffn_cn_b2': _L0_ffn_in['cn_b2'], 'L0_ffn_cn_w3': _L0_ffn_in['cn_w3'], 'L0_ffn_cn_b3': _L0_ffn_in['cn_b3'], 'L0_ffn_cn_w4': _L0_ffn_in['cn_w4'], 'L0_ffn_cn_b4': _L0_ffn_in['cn_b4'], 'L0_ffn_gc_w1': _L0_ffn_in['gc_w1'], 'L0_ffn_gc_b1': _L0_ffn_in['gc_b1'], 'L0_ffn_gc_w2': _L0_ffn_in['gc_w2'], 'L0_ffn_gc_b2': _L0_ffn_in['gc_b2'], 'L0_ffn_gc_w3': _L0_ffn_in['gc_w3'], 'L0_ffn_gc_b3': _L0_ffn_in['gc_b3'], 'L0_ffn_adaptive_range': _L0_ffn_in['adaptive_range']}
    _x0 = _d['L0_attn_x']
    _d['L0_attn_x'] = jax.random.normal(jax.random.fold_in(jax.random.key(seed), 1), (16, 1024, 256), dtype=_x0.dtype)
    del _x0
    return _d

def reference(L0_attn_x, L0_attn_W_in, L0_attn_b_in, L0_attn_W_conv, L0_attn_b_conv, L0_attn_W_x, L0_attn_b_x, L0_attn_W_out, L0_attn_b_out, L0_attn_A_log, L0_attn_D, L0_ffn_cn_w1, L0_ffn_cn_b1, L0_ffn_cn_w2, L0_ffn_cn_b2, L0_ffn_cn_w3, L0_ffn_cn_b3, L0_ffn_cn_w4, L0_ffn_cn_b4, L0_ffn_gc_w1, L0_ffn_gc_b1, L0_ffn_gc_w2, L0_ffn_gc_b2, L0_ffn_gc_w3, L0_ffn_gc_b3, L0_ffn_adaptive_range):

    def _L0_attn_ref(x, W_in, b_in, W_conv, b_conv, W_x, b_x, W_out, b_out, A_log, D):
        import jax, jax.numpy as jnp
        import numpy as np
        from jax import lax
        B, L, DM = (1, 512, 256)
        N = 16
        K = 4
        DI = 2 * DM

        def silu(v):
            return v * jax.nn.sigmoid(v)
        Bsz = x.shape[0]
        xr = x @ W_in.T + b_in
        xi, res = jnp.split(xr, 2, axis=-1)
        xc = jnp.transpose(xi, (0, 2, 1))
        xc = lax.conv_general_dilated(xc, W_conv, window_strides=(1,), padding=[(K - 1, 0)], dimension_numbers=('NCH', 'OIH', 'NCH'), feature_group_count=DI) + b_conv[None, :, None]
        xi = silu(jnp.transpose(xc, (0, 2, 1)))
        proj = xi @ W_x.T + b_x
        delta = jax.nn.softplus(proj[..., :DI])
        B_ssm = proj[..., DI:DI + N]
        C_ssm = proj[..., DI + N:]
        A = -jnp.exp(A_log)
        dA = jnp.exp(delta[..., None] * A)
        dBx = delta[..., None] * B_ssm[:, :, None, :] * xi[..., None]

        def step(h, inp):
            da, dbx, c = inp
            h = da * h + dbx
            y = jnp.einsum('bdn,bn->bd', h, c)
            return (h, y)
        h0 = jnp.zeros((Bsz, DI, N), x.dtype)
        _, ys = lax.scan(step, h0, (jnp.swapaxes(dA, 0, 1), jnp.swapaxes(dBx, 0, 1), jnp.swapaxes(C_ssm, 0, 1)))
        y = jnp.swapaxes(ys, 0, 1) + xi * D
        y = y * silu(res)
        return y @ W_out.T + b_out

    def _L0_ffn_ref(x, cn_w1, cn_b1, cn_w2, cn_b2, cn_w3, cn_b3, cn_w4, cn_b4, gc_w1, gc_b1, gc_w2, gc_b2, gc_w3, gc_b3, adaptive_range):
        import jax, jax.numpy as jnp
        import numpy as np
        B, S, DIM = (4, 1024, 256)
        BASE_COUPLING = 0.1
        NUM_CYCLES = 3

        def _gelu(x):
            return jax.nn.gelu(x, approximate=False)

        def _coupling_net(h, w1, b1, w2, b2, w3, b3, w4, b4):
            h = _gelu(h @ w1 + b1)
            h = _gelu(h @ w2 + b2)
            h = _gelu(h @ w3 + b3)
            return jax.nn.sigmoid(h @ w4 + b4)

        def _global_net(h, w1, b1, w2, b2, w3, b3):
            h = _gelu(h @ w1 + b1)
            h = _gelu(h @ w2 + b2)
            return jax.nn.sigmoid(h @ w3 + b3)

        def _twist(x):
            o_r, o_i, p_r, p_i = jnp.split(x, 4, axis=-1)
            return jnp.concatenate([p_r, -p_i, -o_r, o_i], axis=-1)
        global_context = x.mean(axis=1, keepdims=True)
        gf = _global_net(global_context, gc_w1, gc_b1, gc_w2, gc_b2, gc_w3, gc_b3)
        out = x
        for _ in range(NUM_CYCLES):
            tf = _coupling_net(out, cn_w1, cn_b1, cn_w2, cn_b2, cn_w3, cn_b3, cn_w4, cn_b4)
            combined = 0.7 * gf + 0.3 * tf
            coupling = BASE_COUPLING + adaptive_range * (combined - 0.5) * 2.0
            out = out + coupling * _twist(out)
        return out
    x = L0_attn_x
    x = _layernorm(x + _L0_attn_ref(x, L0_attn_W_in, L0_attn_b_in, L0_attn_W_conv, L0_attn_b_conv, L0_attn_W_x, L0_attn_b_x, L0_attn_W_out, L0_attn_b_out, L0_attn_A_log, L0_attn_D), axis=-1)
    x = _layernorm(x + _L0_ffn_ref(x, L0_ffn_cn_w1, L0_ffn_cn_b1, L0_ffn_cn_w2, L0_ffn_cn_b2, L0_ffn_cn_w3, L0_ffn_cn_b3, L0_ffn_cn_w4, L0_ffn_cn_b4, L0_ffn_gc_w1, L0_ffn_gc_b1, L0_ffn_gc_w2, L0_ffn_gc_b2, L0_ffn_gc_w3, L0_ffn_gc_b3, L0_ffn_adaptive_range), axis=-1)
    return x

_drawn_inputs = setup_inputs


def setup_inputs(seed=0):
    import zlib

    import numpy as np

    out = dict(_drawn_inputs(seed))
    spreads = {'L0_attn_b_in': (0.0, 0.8),
     'L0_attn_b_conv': (0.0, 0.8),
     'L0_attn_b_x': (0.0, 0.8),
     'L0_attn_b_out': (0.0, 0.8),
     'L0_attn_D': (1.0, 0.6),
     'L0_ffn_cn_b1': (0.0, 2.0),
     'L0_ffn_cn_b2': (0.0, 2.0),
     'L0_ffn_cn_b3': (0.0, 2.0),
     'L0_ffn_gc_b1': (0.0, 0.8),
     'L0_ffn_gc_b2': (0.0, 0.8)}
    factors = {'L0_attn_W_in': 8.0,
     'L0_attn_W_conv': 8.0,
     'L0_attn_W_x': 8.0,
     'L0_attn_W_out': 8.0,
     'L0_attn_A_log': 8.0,
     'L0_ffn_cn_w1': 7.45,
     'L0_ffn_cn_w2': 7.71,
     'L0_ffn_cn_w3': 6.084,
     'L0_ffn_cn_w4': 6.985,
     'L0_ffn_gc_w1': 8.0,
     'L0_ffn_gc_w2': 8.0,
     'L0_ffn_gc_w3': 5.294}
    for name, (base, spread) in spreads.items():
        noise = np.random.default_rng([zlib.crc32(name.encode()), seed]).standard_normal(out[name].shape)
        drawn = base * np.exp(spread * noise) if base else spread * noise
        out[name] = jnp.asarray(drawn.astype(out[name].dtype))
    for name, factor in factors.items():
        out[name] = (out[name] * factor).astype(out[name].dtype)
    return out
```

```python
from contextlib import ExitStack

import concourse.bass as bass
from concourse import mybir

ALU = mybir.AluOpType
ACT = mybir.ActivationFunctionType
F32 = mybir.dt.float32

P = 128
BATCH, SEQ, DM = 16, 1024, 256
DI, NS, TAPS = 512, 16, 4
L = 512
CH = SEQ // L
DC = DI // P
NP = NS // 2
SLOTS = CH * DC
POINTS = SLOTS * NP
HALO = TAPS - 1
EPS = 1e-5
LN_EXP = "natural_log_exp_and_others"

POOL_PAIRS = (3,)
DVE_PAIRS = tuple(p for p in range(NP) if p not in POOL_PAIRS)
DBX_RING = 4
PROD_RING = 2

W_COLS = {}
_at = 0
for _name, _n in (("in", 2 * 2 * DI), ("x", 4 * (DI + 2 * NS)), ("out", 4 * DM), ("w1", 2 * 256),
                  ("w2", 2 * 128), ("w3", 64), ("w4", P), ("g1", 2 * 128), ("g2", 64), ("g3", P)):
    W_COLS[_name] = (_at, _at + _n)
    _at += _n
W_TOTAL = _at
V_COLS = {}
_at = 0
for _name, _n in (("b_in", 8), ("b_conv", 4), ("w_conv", 16), ("b_x", 4), ("D", 4), ("A", 64),
                  ("b_bc", 1), ("b1", 2), ("b2", 1), ("b3", 1), ("b4", 1), ("gb1", 1), ("gb2", 1),
                  ("gb3", 1), ("range", 1), ("sign", 1), ("eye", P), ("b_out", DM)):
    V_COLS[_name] = (_at, _at + _n)
    _at += _n
V_TOTAL = _at

PROJ = []
for _h in range(CH):
    for _s, _kinds in enumerate((("delta", "res", "xi", "xi"), ("delta", "res", "xi", "xi"),
                                 ("delta", "res", "bc"), ("delta", "res"))):
        PROJ += [(DC * _h + _s, _k) for _k in _kinds]
PROJ_LAST = [t for t in PROJ if t[0] < DC or t[1] == "res" or t[1] == "delta" and t[0] < SLOTS - 1]
PROJ_FIRST = 6
PROJ_PAIR = {"delta": 0, "res": 1, "bc": 6}
XI_PAIRS = (3, 5)

CYCLES = 3
F_PER = 10
F_AT = (0, 1, 2, 3, 5, 6, 8, 9, 11, 12)
GELU_AT = (6, 9, 12)
TANH_AT = 15
MULT_AT = 17
UPD_AT = 15
G_AT = (4, 8, 11)
T_AT = (3, 4, 6, 7)
E_AT = (56, 57, 58, 59)
O_AT = {1: (1, 2), 0: (34, 37)}


COPY_LAG = 3
STATS_LAG, NORM_LAG, RSTD_LAG = 2, 4, 5
XI_TAKEN = (6, 8)
XI_CONV = (6, 8)
XI_HALO = (8, 10)


def late(q):
    return min(q, POINTS - 1)


def xi_of(q, at):
    for s in range(SLOTS):
        for n in range(2):
            if s % DC < 2 and NP * s + at[n] == q:
                return 2 * (s % DC) + n, s
    return None


def cycle_at(c):
    return NP + 2 * NP * c


def silu_pair(s):
    return 5 if s in (2, 4, 6) else 4


def bank_tasks(main, coupling):
    tasks = []
    if coupling:
        tasks += [(q, "t", n) for n, q in enumerate(T_AT)] + [(q, "e", n) for n, q in enumerate(E_AT)]
        tasks += [(q, "o", n - 2) for n, q in enumerate(O_AT[1])]
        tasks += [(cycle_at(c) + q, "f", F_PER * c + n) for c in range(CYCLES) for n, q in enumerate(F_AT)]
        tasks += [(cycle_at(0) + q, "g", n) for n, q in enumerate(G_AT)]
    if main:
        tasks += [(q, "o", n) for n, q in enumerate(O_AT[0])]
    return sorted(tasks)


def dve_products(q):
    return len(DVE_PAIRS) * (q // NP) + sum(p in DVE_PAIRS for p in range(q % NP + 1))


def proj_index(s, kind, nth=0, tasks=PROJ):
    return [i for i, t in enumerate(tasks) if t == (s, kind)][nth]


def counts(n):
    return not isinstance(n, int) or n > 0


def build(nc, x, xT, weights, vectors, out):
    x1_dram = nc.dram_tensor("x1_scratch", [BATCH, SEQ, DM], F32, kind="Internal").ap()
    bc_dram = nc.dram_tensor("bc_scratch", [CH, 2, NS, L], F32, kind="Internal").ap()

    with ExitStack() as ctx:
        def sb(name, shape):
            return ctx.enter_context(nc.sbuf_tensor(name, shape, F32))

        def psum(name, shape):
            return ctx.enter_context(nc.psum_tensor(name, shape, F32))

        def sem(name):
            return ctx.enter_context(nc.semaphore(name))

        w_all = sb("w_all", [P, W_TOTAL])
        v_all = sb("v_all", [P, V_TOTAL])
        x_feat = sb("x_feat", [P, CH, 2, L])
        x_res = sb("x_res", [P, 4, DM])
        pre = sb("pre", [P, 2, HALO + L])
        halo = sb("halo", [P, DC, HALO])
        xi = sb("xi", [P, CH, DC, L])
        s_res = sb("s_res", [P, 2, L])
        delta = sb("delta", [P, 2, L])
        log_part = sb("log_part", [P, L])
        u = sb("u", [P, 2, L])
        bc_rows = sb("bc_rows", [2 * NS, L])
        bc = sb("bc", [P, NP, 2, 2, L])
        dbx = sb("dbx", [P, DBX_RING, 2, L])
        h_pool = sb("h_pool", [P, 2, L])
        prod = sb("prod", [P, PROD_RING, 2, L])
        carry = sb("carry", [P, DC * NS])
        yg = sb("yg", [P, DC, L])
        x1 = sb("x1", [P, CH, 4, DM])
        stats = sb("stats", [P, 2, 2, 6])
        mean_var = sb("mean_var", [P, 2, 2, 2])
        log_var = sb("log_var", [P, 2, 2])
        r_std = sb("r_std", [P, 2, 2])
        eps_col = sb("eps_col", [P, 1])
        oT = sb("oT", [P, 2, SEQ])
        big = sb("big", [P, 2, SEQ])
        mid = sb("mid", [P, SEQ])
        sums = sb("sums", [P, 4])
        g_act = sb("g_act", [P, 3])
        neg_a = sb("neg_a", [P, DC * NS])
        conv_bias = sb("conv_bias", [P, DC])
        half_b4 = sb("half_b4", [P, 2])
        coef = sb("coef", [P, 4])

        def w(name, k, n, rows=P):
            a, _ = W_COLS[name]
            return w_all[0:rows, a:a + k * n].rearrange("p (k n) -> p k n", k=k)

        def v(name, c=0, rows=P):
            a, _ = V_COLS[name]
            return v_all[0:rows, a + c:a + c + 1]

        def vs(name):
            a, e = V_COLS[name]
            return v_all[:, a:e]

        w_in, w_x, w_out = w("in", 2, 2 * DI), w("x", 4, DI + 2 * NS), w("out", 4, DM)
        w1, w2, w3 = w("w1", 2, 256), w("w2", 2, 128), w("w3", 1, 64)
        w4 = w("w4", 1, P, 64)
        g1, g2, g3 = w("g1", 2, 128), w("g2", 1, 64), w("g3", 1, P, 64)
        eye, b_out = vs("eye"), vs("b_out")
        residual = big[:, :, :].rearrange("p m t -> p (m t)").rearrange("p (k c) -> p k c", c=DM)

        da = psum("da", [P, 2, 2, L])
        y_sum = psum("y_sum", [P, L])
        proj = psum("proj", [P, 2, L])
        shared = psum("shared", [P, L])

        w_in_sem = sem("weights_loaded")
        v_in_sem = sem("vectors_loaded")
        xf_in = [sem(f"x_feat_loaded{i}") for i in range(CH)]
        xr_in = sem("x_res_loaded")
        bc_in = [sem(f"bc_loaded{i}") for i in range(NP)]
        bc_stored = sem("bc_stored")
        x1_stored = [sem(f"x1_stored{i}") for i in range(CH)]
        re_in = sem("residual_loaded")
        out_done = sem("out_stored")
        act_setup = sem("act_setup")
        pool_setup = sem("pool_setup")
        proj_ready = sem("proj_ready")
        proj_taken = sem("proj_taken")
        sp_step = sem("softplus_step")
        log_ready = sem("log_ready")
        delta_ready = sem("delta_ready")
        u_ready = sem("u_ready")
        halo_ready = sem("halo_ready")
        conv_step = sem("conv_step")
        xi_ready = sem("xi_ready")
        da_ready = sem("da_ready")
        dbx_ready = sem("dbx_ready")
        scans = sem("scans_done")
        carried = sem("carried")
        prod_dve = sem("products_by_vector")
        prod_pool = sem("products_by_gpsimd")
        prod_used = sem("products_used")
        y_ready = sem("y_ready")
        y_taken = sem("y_taken")
        gated = sem("gated")
        xb_ready = sem("residual_with_bias")
        o_ready, o_sum, o_stat, o_mv, o_rstd, o_norm = (sem("o_" + n) for n in
                                                        ("ready", "sum", "stat", "mv", "rstd", "norm"))
        e_ready, e_sum, e_stat, e_mv, e_rstd, e_norm = (sem("e_" + n) for n in
                                                        ("ready", "sum", "stat", "mv", "rstd", "norm"))
        o_log, e_log = sem("o_log"), sem("e_log")
        t_ready, t_taken = sem("t_ready"), sem("t_taken")
        f_ready, f_taken, f_gelu, f_tanh = sem("f_ready"), sem("f_taken"), sem("f_gelu"), sem("f_tanh")
        g_ready, g_taken, g_actd = sem("g_ready"), sem("g_taken"), sem("g_activated")
        alpha_ready, cs_ready, cprod_ready, updated = (sem(n) for n in (
            "alpha_ready", "coupling_ready", "coupling_products", "updated"))

        TAKEN = {"t": (t_taken, 4, 0), "f": (f_taken, CYCLES * F_PER, 0), "g": (g_taken, 3, 0),
                 "o": (o_sum, 4, 1), "e": (e_sum, 4, 0)}

        block = ctx.enter_context(nc.Block(no_gpsimd_drain=True))

        def in_register(eng, n):
            return n if isinstance(n, int) else eng.to_reg(n)

        def each_batch(eng, body):
            body(0)
            body(1)
            with eng.Fori(2, BATCH - 1) as b:
                body(b)
            body(BATCH - 1)
            body(BATCH)

        def kinds(b):
            if not isinstance(b, int):
                return True, True, True
            return b < BATCH, b > 0, b < BATCH - 1

        @block.sync
        def _(sp):
            def load_x_feat(b, h):
                sp.dma_start(x_feat[:, h], xT[b].rearrange("(k p) t -> p k t", p=P)[:, :, h * L:(h + 1) * L]) \
                  .then_inc(xf_in[h], 16)

            def store_bc(h):
                sp.dma_start(bc_dram[h].rearrange("a n t -> (a n) t"), bc_rows[:, :]).then_inc(bc_stored, 16)

            def load_bc(h, p):
                sp.dma_start(bc[:, p], bc_dram[h, :, 2 * p:2 * p + 2, :].partition_broadcast(P)) \
                  .then_inc(bc_in[p], 16)

            sp.dma_start(v_all[:, :], vectors).then_inc(v_in_sem, 16)
            load_x_feat(0, 0)
            sp.dma_start(w_all[:, :], weights).then_inc(w_in_sem, 16)
            load_x_feat(0, 1)
            sp.wait_ge(proj_taken, 5)
            store_bc(0)
            sp.wait_ge(bc_stored, 16)
            for p in range(NP):
                load_bc(0, p)

            def body(b):
                main, before, after = kinds(b)
                for h in range(CH):
                    if main:
                        if counts(count := b * 4 + 2 * h):
                            count = in_register(sp, count)
                            sp.wait_ge(v_in_sem, 16)
                            sp.wait_ge(o_sum, count)
                        sp.dma_start(x_res[:, :, :], x[b, h * L:(h + 1) * L, :].rearrange("(k p) c -> p k c", p=P)) \
                          .then_inc(xr_in, 16)
                    if h == 0 and before:
                        count = in_register(sp, b * 4)
                        sp.wait_ge(v_in_sem, 16)
                        sp.wait_ge(o_norm, count)
                        sp.dma_start(x1_dram[b - 1, L:SEQ, :].rearrange("(k p) c -> p k c", p=P), x1[:, 1]) \
                          .then_inc(x1_stored[1], 16)
                    if h == 1 and main:
                        count = in_register(sp, b * 4 + 2)
                        sp.wait_ge(v_in_sem, 16)
                        sp.wait_ge(o_norm, count)
                        sp.dma_start(x1_dram[b, 0:L, :].rearrange("(k p) c -> p k c", p=P), x1[:, 0]) \
                          .then_inc(x1_stored[0], 16)
                    if h == 1 and before:
                        count = in_register(sp, b * 16)
                        sp.wait_ge(v_in_sem, 16)
                        sp.wait_ge(x1_stored[0], count)
                        count = in_register(sp, b * 16)
                        sp.wait_ge(v_in_sem, 16)
                        sp.wait_ge(x1_stored[1], count)
                        count = in_register(sp, b * CYCLES)
                        sp.wait_ge(v_in_sem, 16)
                        sp.wait_ge(updated, count)
                        sp.dma_start(residual, x1_dram[b - 1].rearrange("(k p) c -> p k c", p=P)) \
                          .then_inc(re_in, 16)
                    if main and (h == 0 or after):
                        nh = 1 - h
                        count = in_register(sp, b * len(PROJ) + PROJ_FIRST + proj_index(DC * h + 2, "bc") + 1)
                        sp.wait_ge(v_in_sem, 16)
                        sp.wait_ge(proj_taken, count)
                        store_bc(nh)
                        count = in_register(sp, b * 32 + 16 * (h + 2))
                        sp.wait_ge(v_in_sem, 16)
                        sp.wait_ge(bc_stored, count)
                        for p in range(NP):
                            q = (DC * h + DC - 1) * NP + p
                            count = in_register(sp, b * POINTS + q + 1)
                            sp.wait_ge(v_in_sem, 16)
                            sp.wait_ge(dbx_ready, count)
                            if p in POOL_PAIRS:
                                count = in_register(sp, b * SLOTS + DC * h + DC)
                                sp.wait_ge(v_in_sem, 16)
                                sp.wait_ge(prod_pool, count)
                            else:
                                count = in_register(sp, b * dve_products(POINTS - 1) + dve_products(q))
                                sp.wait_ge(v_in_sem, 16)
                                sp.wait_ge(prod_dve, count)
                            load_bc(nh, p)
                        if h == 0 and after or h == 1 and after:
                            count = in_register(sp, b * len(PROJ) + PROJ_FIRST + proj_index(DC * h + DC - 1, "res") + 1)
                            sp.wait_ge(v_in_sem, 16)
                            sp.wait_ge(proj_ready, count)
                            load_x_feat(b + 1, h)
                    if h == 1 and before:
                        for i in range(CH):
                            count = in_register(sp, b * 4 - 4 + 2 * i + 2)
                            sp.wait_ge(v_in_sem, 16)
                            sp.wait_ge(e_norm, count)
                            sp.dma_start(out[b - 1, i * L:(i + 1) * L, :].rearrange("(k p) c -> p k c", p=P),
                                         residual[:, 4 * i:4 * i + 4, :]).then_inc(out_done, 16)

            each_batch(sp, body)
            sp.wait_ge(out_done, BATCH * CH * 16)
            for i in range(CH):
                sp.wait_ge(x1_stored[i], BATCH * 16)
            sp.wait_ge(bc_stored, BATCH * CH * 16)

        @block.tensor
        def _(pe):
            def proj_in(bank, h, col):
                for k in range(2):
                    mm = pe.matmul(proj[:, bank, :], w_in[:, k, col:col + P], x_feat[:, h, k, :],
                                   start=k == 0, stop=k == 1)
                mm.then_inc(proj_ready, 1)

            def proj_x(bank, h, col, n):
                for k in range(4):
                    mm = pe.matmul(proj[0:n, bank, :], w_x[:, k, col:col + n], xi[:, h, k, :],
                                   start=k == 0, stop=k == 3)
                mm.then_inc(proj_ready, 1)

            pe.wait_ge(v_in_sem, 16)
            pe.wait_ge(w_in_sem, 16)
            pe.wait_ge(xf_in[0], 16)
            for m in range(DC):
                if counts(count := m - 1):
                    pe.wait_ge(proj_taken, count)
                proj_in(m % 2, 0, m * P)
            pe.wait_ge(proj_taken, 3)
            pe.wait_ge(xi_ready, DC)
            proj_x(0, 0, DI, 2 * NS)
            pe.wait_ge(proj_taken, 4)
            proj_x(1, 0, 0, P)

            def run_proj(b, tasks, i):
                s, kind = tasks[i]
                h = s // DC
                pe.wait_ge(proj_taken, b * len(PROJ) + PROJ_FIRST + i - 1)
                if kind == "delta":
                    n = (s + 1) % SLOTS
                    if n % DC == 0:
                        pe.wait_ge(xi_ready, b * CH * DC + DC * (h + 2))
                    proj_x(i % 2, n // DC, (n % DC) * P, P)
                elif kind == "res":
                    proj_in(i % 2, h, DI + (s % DC) * P)
                elif kind == "xi":
                    m = 2 * (s % DC) + (i - proj_index(s, "xi", 0, tasks))
                    if m == 0:
                        pe.wait_ge(xf_in[1 - h], b * 16 + 16 * (1 + h))
                    proj_in(i % 2, 1 - h, m * P)
                else:
                    pe.wait_ge(xi_ready, b * CH * DC + DC * (h + 2))
                    proj_x(i % 2, 1 - h, DI, 2 * NS)

            def run_shared(b, kind, n, before_it):
                if before_it is not None:
                    pk, pn, lag = before_it
                    s_, per, own = TAKEN[pk]
                    pe.wait_ge(s_, b * per + pn + 1 - (0 if own else per) - lag * per)
                if kind == "t":
                    half, m = n // 2, n % 2
                    pe.wait_ge(o_norm, b * 4 - 4 + 2 * half + 2)
                    for k in range(4):
                        mm = pe.transpose(shared[:, k * P:(k + 1) * P], x1[:, half, k, m * P:(m + 1) * P], eye)
                    mm.then_inc(t_ready, 1)
                elif kind == "o":
                    i = n % 2
                    h = 0 if n >= 0 else 1
                    pe.wait_ge(gated, b * SLOTS + (DC if h == 0 else 0))
                    for r in range(2):
                        tb = 2 * i + r
                        for k in range(4):
                            mm = pe.matmul(shared[:, r * DM:(r + 1) * DM], yg[:, k, tb * P:(tb + 1) * P],
                                           w_out[:, k, :], start=k == 0, stop=k == 3)
                    mm.then_inc(o_ready, 1)
                elif kind == "e":
                    half, i = n // 2, n % 2
                    pe.wait_ge(updated, b * CYCLES)
                    for r in range(2):
                        for m in range(2):
                            t0 = half * L + (2 * i + r) * P
                            mm = pe.transpose(shared[:, r * DM + m * P:r * DM + (m + 1) * P],
                                              oT[:, m, t0:t0 + P], eye)
                    mm.then_inc(e_ready, 1)
                elif kind == "g":
                    if n == 0:
                        pe.wait_ge(t_taken, b * 4)
                        for m in range(2):
                            for half in range(2):
                                mm = pe.matmul(shared[:, 0:1], g1[:, m, :], sums[:, 2 * m + half:2 * m + half + 1],
                                               start=m + half == 0, stop=m + half == 2)
                    elif n == 1:
                        pe.wait_ge(g_actd, b * 3 - 3 + 1)
                        mm = pe.matmul(shared[0:64, 0:1], g2[:, 0, :], g_act[:, 0:1], start=True, stop=True)
                    else:
                        pe.wait_ge(g_actd, b * 3 - 3 + 2)
                        mm = pe.matmul(shared[:, 0:1], g3[:, 0, :], g_act[0:64, 1:2], start=True, stop=True)
                    mm.then_inc(g_ready, 1)
                else:
                    c, n = n // F_PER, n % F_PER
                    if n < 4:
                        half, m = n // 2, n % 2
                        if c:
                            pe.wait_ge(updated, b * CYCLES - CYCLES + c)
                        elif m == 0:
                            pe.wait_ge(t_taken, b * 4 - 4 + 2 * half + 2)
                        for k in range(2):
                            mm = pe.matmul(shared[:, :], w1[:, k, m * P:(m + 1) * P],
                                           oT[:, k, half * L:(half + 1) * L], start=k == 0, stop=k == 1)
                    else:
                        stage, half = (n - 4) // 2, n % 2
                        if half == 0:
                            pe.wait_ge(f_gelu, b * 9 - 9 + 3 * c + stage + 1)
                        t = slice(half * L, (half + 1) * L)
                        if stage == 0:
                            for k in range(2):
                                mm = pe.matmul(shared[:, :], w2[:, k, :], big[:, k, t], start=k == 0, stop=k == 1)
                        elif stage == 1:
                            mm = pe.matmul(shared[0:64, :], w3[:, 0, :], mid[:, t], start=True, stop=True)
                        else:
                            mm = pe.matmul(shared[:, :], w4[:, 0, :], big[0:64, 0, t], start=True, stop=True)
                    mm.then_inc(f_ready, 1)

            def add_pair(b, s, src, first, last, done):
                for k in range(2):
                    mm = pe.matmul(y_sum[:, :], eye, src[:, k, :], start=first and k == 0, stop=last and k == 1)
                    if k == 1:
                        mm.then_inc(done, 1)

            def body(b):
                main, before, after = kinds(b)
                tasks = bank_tasks(main, before)
                if isinstance(b, int) and b == 0:
                    last = None
                elif isinstance(b, int) and b == 1:
                    last = ("o", 1, 1)
                else:
                    last = ("e", 3, 1)
                for q in range(POINTS):
                    s, p = q // NP, q % NP
                    h = s // DC
                    if main:
                        if p in DVE_PAIRS:
                            if p == DVE_PAIRS[0]:
                                if counts(count := b * SLOTS + s):
                                    pe.wait_ge(y_taken, count)
                            pe.wait_ge(prod_dve, b * dve_products(POINTS - 1) + dve_products(q))
                            add_pair(b, s, prod[:, (dve_products(q) - 1) % PROD_RING], p == DVE_PAIRS[0],
                                     p == NP - 1 and not POOL_PAIRS,
                                     y_ready if p == NP - 1 and not POOL_PAIRS else prod_used)
                        if p == NP - 1 and POOL_PAIRS:
                            pe.wait_ge(prod_pool, b * SLOTS + s + 1)
                            add_pair(b, s, h_pool, False, True, y_ready)
                        projections = PROJ if after else PROJ_LAST
                        for i, (ps, kind) in enumerate(projections):
                            if ps != s:
                                continue
                            at = XI_PAIRS[i - proj_index(s, "xi", 0, projections)] if kind == "xi" else PROJ_PAIR[kind]
                            if at == p:
                                run_proj(b, projections, i)
                    for tq, kind, n in tasks:
                        if tq == q:
                            run_shared(b, kind, n, last)
                            last = (kind, n, 0)

            each_batch(pe, body)

        @block.scalar
        def _(act):
            def take_xi(bank, h, m, c):
                if counts(count := c * 3 - 3):
                    act.wait_ge(conv_step, count)
                if counts(count := c - 1):
                    act.wait_ge(halo_ready, count)
                act.activation(xi[:, h, m, :], proj[:, bank, :], ACT.Identity,
                               bias=conv_bias[:, m:m + 1], scale=v("w_conv", m * TAPS + TAPS - 1))
                act.activation(pre[:, m % 2, HALO:], proj[:, bank, :], ACT.Identity,
                               bias=v("b_in", m), scale=1.0).then_inc(proj_taken, 1)

            def take_delta(bank, dc, par, n):
                if counts(count := n):
                    act.wait_ge(u_ready, count)
                act.activation(log_part[:, :], proj[:, bank, :], ACT.Abs, bias=v("b_x", dc), scale=1.0) \
                   .then_inc(sp_step, 1)
                act.activation(delta[:, par, :], proj[:, bank, :], ACT.Relu, bias=v("b_x", dc), scale=1.0) \
                   .then_inc(proj_taken, 1)
                act.wait_ge(sp_step, n * 2 + 1)
                act.activation(log_part[:, :], log_part[:, :], ACT.Exp, scale=-1.0).then_inc(sp_step, 1)
                act.wait_ge(sp_step, n * 2 + 2)
                act.activation(log_part[:, :], log_part[:, :], ACT.Ln, bias=1.0, scale=1.0).then_inc(log_ready, 1)

            def r_stds(mv, log_done, rs, n, i):
                act.wait_ge(mv, n + 1)
                act.activation(log_var[:, i, :], mean_var[:, i, :, 1], ACT.Ln, bias=eps_col[:, 0:1], scale=1.0) \
                   .then_inc(log_done, 1)
                act.wait_ge(log_done, n + 1)
                act.activation(r_std[:, i, :], log_var[:, i, :], ACT.Exp, scale=-0.5).then_inc(rs, 1)

            act.wait_ge(v_in_sem, 16)
            nc.scalar.preload_act_table_set(LN_EXP)
            act.activation(neg_a[:, :], vs("A"), ACT.Exp).then_inc(act_setup, 1)
            act.wait_ge(pool_setup, 5)
            for m in range(DC):
                act.wait_ge(proj_ready, m + 1)
                if m >= 2:
                    act.wait_ge(conv_step, 3 * (m - 1))
                    act.wait_ge(halo_ready, m - 1)
                take_xi(m % 2, 0, m, 0)
            for m in range(DC):
                act.wait_ge(conv_step, 3 * m + 3)
                act.activation(xi[:, 0, m, :], xi[:, 0, m, :], ACT.Silu).then_inc(xi_ready, 1)
            nc.scalar.preload_act_table_set(LN_EXP)
            act.wait_ge(proj_ready, 5)
            act.activation(bc_rows[:, :], proj[0:2 * NS, 0, :], ACT.Identity,
                           bias=v("b_bc", 0, 2 * NS), scale=1.0).then_inc(proj_taken, 1)
            act.wait_ge(proj_ready, 6)
            take_delta(1, 0, 0, 0)

            def body(b):
                main, before, after = kinds(b)
                for q in range(POINTS):
                    s, p = q // NP, q % NP
                    h, dc = s // DC, s % DC
                    projections = PROJ if after else PROJ_LAST
                    if main:
                        if p == 0:
                            act.wait_ge(delta_ready, b * SLOTS + s + 1)
                        if counts(count := b * 2 * POINTS + 2 * q - 2):
                            act.wait_ge(scans, count)
                        if (p - 2) % NP in DVE_PAIRS:
                            if counts(count := b * dve_products(POINTS - 1) + dve_products(q - 2)):
                                act.wait_ge(prod_dve, count)
                        for k in range(2):
                            n = 2 * p + k
                            e = act.activation(da[:, q % 2, k, :], delta[:, s % 2, :], ACT.Exp,
                                               scale=neg_a[:, dc * NS + n:dc * NS + n + 1])
                        e.then_inc(da_ready, 1)
                    if main and p == 3 and (s < SLOTS - 1 or after):
                        i = proj_index(s, "delta", 0, projections)
                        act.wait_ge(proj_ready, b * len(PROJ) + PROJ_FIRST + i + 1)
                        n = (s + 1) % SLOTS
                        take_delta(i % 2, n % DC, n % 2, b * SLOTS + s + 1)
                    if main and p == 1 and dc == 3 and (h == 0 or after):
                        i = proj_index(s - 1, "bc")
                        act.wait_ge(proj_ready, b * len(PROJ) + PROJ_FIRST + i + 1)
                        act.wait_ge(bc_stored, b * 32 + 16 * (h + 1))
                        act.activation(bc_rows[:, :], proj[0:2 * NS, i % 2, :], ACT.Identity,
                                       bias=v("b_bc", 0, 2 * NS), scale=1.0).then_inc(proj_taken, 1)
                    for tq, kind, n in (bank_tasks(main, before) if before else []):
                        if tq + COPY_LAG != q or kind in ("o", "e"):
                            continue
                        if kind == "t":
                            half, m = n // 2, n % 2
                            act.wait_ge(t_ready, b * 4 - 4 + n + 1)
                            if counts(count := b * 4 - 4):
                                act.wait_ge(e_ready, count)
                            act.activation(oT[:, m, half * L:(half + 1) * L], shared[:, :], ACT.Identity,
                                           accum_out=sums[:, 2 * m + half:2 * m + half + 1]).then_inc(t_taken, 1)
                        elif kind == "g":
                            rows = 64 if n == 1 else P
                            act.wait_ge(g_ready, b * 3 - 3 + n + 1)
                            act.activation(g_act[0:rows, n:n + 1], shared[0:rows, 0:1], ACT.Identity,
                                           bias=v(("gb1", "gb2", "gb3")[n], 0, rows),
                                           scale=1.0 / SEQ if n == 0 else 1.0).then_inc(g_taken, 1)
                        else:
                            c, task = n // F_PER, n % F_PER
                            act.wait_ge(f_ready, (b * 3 - 3) * F_PER + n + 1)
                            if task < 4:
                                half, m = task // 2, task % 2
                                if task == 0 and c == 0:
                                    if counts(count := b * 32 - 32):
                                        act.wait_ge(out_done, count)
                                elif task == 0:
                                    act.wait_ge(updated, b * CYCLES - CYCLES + c)
                                dst, bias, rows = big[:, m, half * L:(half + 1) * L], v("b1", m), P
                            else:
                                stage, half = (task - 4) // 2, task % 2
                                t = slice(half * L, (half + 1) * L)
                                dst, bias, rows = ((mid[:, t], v("b2"), P), (big[0:64, 0, t], v("b3", 0, 64), 64),
                                                   (mid[:, t], v("b4"), P))[stage]
                            act.activation(dst, shared[0:rows, :], ACT.Identity, bias=bias, scale=1.0) \
                               .then_inc(f_taken, 1)
                    for hh, use in ((1, before), (0, main)):
                        for i in range(2):
                            if use and q == O_AT[hh][i] + RSTD_LAG:
                                r_stds(o_mv, o_log, o_rstd, b * 4 + i - (2 if hh else 0), i)
                    for e in range(4 if before else 0):
                        if q == late(E_AT[e] + RSTD_LAG):
                            r_stds(e_mv, e_log, e_rstd, b * 4 - 4 + e, e % 2)
                    switched = False
                    if main and p == silu_pair(s):
                        i = proj_index(s, "res", 0, projections)
                        act.wait_ge(proj_ready, b * len(PROJ) + PROJ_FIRST + i + 1)
                        if counts(count := b * SLOTS + s - 1):
                            act.wait_ge(gated, count)
                        act.activation(s_res[:, s % 2, :], proj[:, i % 2, :], ACT.Silu,
                                       bias=v("b_in", DC + dc), scale=1.0).then_inc(proj_taken, 1)
                        if dc in (1, 2) and (h == 0 or after):
                            for m in (2 * dc - 2, 2 * dc - 1):
                                act.wait_ge(conv_step, b * 24 + 12 * h + 12 + 3 * m + 3)
                                act.activation(xi[:, 1 - h, m, :], xi[:, 1 - h, m, :], ACT.Silu) \
                                   .then_inc(xi_ready, 1)
                        switched = True
                    for c in range(CYCLES if before else 0):
                        at = q - cycle_at(c)
                        taken = (b * 3 - 3 + c) * F_PER
                        if at == GELU_AT[0]:
                            act.wait_ge(f_taken, taken + 4)
                            act.activation(big[:, :, :], big[:, :, :], ACT.Gelu).then_inc(f_gelu, 1)
                            switched = True
                        if at == GELU_AT[1]:
                            act.wait_ge(f_taken, taken + 6)
                            act.activation(mid[:, :], mid[:, :], ACT.Gelu).then_inc(f_gelu, 1)
                            switched = True
                        if at == GELU_AT[2]:
                            act.wait_ge(f_taken, taken + 8)
                            act.activation(big[0:64, 0, :], big[0:64, 0, :], ACT.Gelu).then_inc(f_gelu, 1)
                            switched = True
                        if c == 0 and at in GELU_AT[1:]:
                            n = GELU_AT.index(at) - 1
                            rows = 64 if n == 1 else P
                            act.wait_ge(g_taken, b * 3 - 3 + n + 1)
                            act.activation(g_act[0:rows, n:n + 1], g_act[0:rows, n:n + 1], ACT.Gelu) \
                               .then_inc(g_actd, 1)
                        if at == TANH_AT:
                            if c == 0:
                                act.wait_ge(g_taken, b * 3)
                                act.activation(g_act[:, 2:3], g_act[:, 2:3], ACT.Tanh, scale=0.5).then_inc(g_actd, 1)
                            act.wait_ge(f_taken, taken + 10)
                            act.activation(mid[:, :], mid[:, :], ACT.Tanh, scale=0.5).then_inc(f_tanh, 1)
                            switched = True
                    if switched and (main or q < POINTS - 1):
                        nc.scalar.preload_act_table_set(LN_EXP)
                    if main and xi_of(q, XI_TAKEN) and (h == 0 or after):
                        m, xs = xi_of(q, XI_TAKEN)
                        i = proj_index(xs, "xi", m % 2)
                        act.wait_ge(proj_ready, b * len(PROJ) + PROJ_FIRST + i + 1)
                        if m == 0:
                            if counts(count := b * SLOTS + DC * h):
                                act.wait_ge(y_taken, count)
                        take_xi(i % 2, 1 - h, m, b * CH * DC + DC * h + DC + m)

            each_batch(act, body)

        @block.vector
        def _(dve):
            def convolve(h, m, c):
                for k in range(HALO):
                    if k:
                        dve.wait_ge(conv_step, c * 3 + k)
                    dve.scalar_tensor_tensor(out=xi[:, h, m, :], in0=pre[:, m % 2, k:k + L],
                                             scalar=v("w_conv", m * TAPS + k), in1=xi[:, h, m, :],
                                             op0=ALU.mult, op1=ALU.add).then_inc(conv_step, 1)

            def norm_stats(sums_, st, mv, n, i, dst):
                dve.wait_ge(sums_, n + 1)
                for r in range(2):
                    ins = dve.bn_stats(stats[:, i, r, :], dst[:, r, :])
                ins.then_inc(st, 1)
                count = in_register(dve, n + 1)
                dve.wait_ge(v_in_sem, 16)
                dve.wait_ge(st, count)
                for r in range(2):
                    ins = dve.bn_aggr(mean_var[:, i, r, :], stats[:, i, r, :])
                ins.then_inc(mv, 1)

            def normalise(rs, done, n, i, dst):
                dve.wait_ge(rs, n + 1)
                for r in range(2):
                    ins = dve.tensor_scalar(dst[:, r, :], dst[:, r, :], mean_var[:, i, r, 0:1], r_std[:, i, r:r + 1],
                                            ALU.subtract, ALU.mult)
                ins.then_inc(done, 1)

            for m in range(DC):
                dve.wait_ge(proj_taken, m + 1)
                dve.wait_ge(halo_ready, m + 1)
                convolve(0, m, m)

            def take_y(b, s):
                h, dc = (s // DC) % CH, s % DC
                dve.wait_ge(y_ready, b * SLOTS + s + 1)
                if dc == 0:
                    if counts(count := b * 4 + 2 * h):
                        dve.wait_ge(o_ready, count)
                dve.scalar_tensor_tensor(out=yg[:, dc, :], in0=xi[:, h, dc, :], scalar=v("D", dc), in1=y_sum[:, :],
                                         op0=ALU.mult, op1=ALU.add).then_inc(y_taken, 1)

            def body(b):
                main, before, after = kinds(b)
                for q in range(POINTS):
                    s, p = q // NP, q % NP
                    h, dc = s // DC, s % DC
                    tile = da[:, q % 2]
                    if main:
                        dve.wait_ge(da_ready, b * POINTS + q + 1)
                        dve.wait_ge(dbx_ready, b * POINTS + q + 1)
                        if p in POOL_PAIRS:
                            if counts(count := b * SLOTS + s):
                                dve.wait_ge(y_ready, count)
                        for k in range(2):
                            n = dc * NS + 2 * p + k
                            if h == 1 and k == 0:
                                dve.wait_ge(carried, b * DC * NP + dc * NP + p + 1)
                            dst = h_pool[:, k, :] if p in POOL_PAIRS else tile[:, k, :]
                            dve.tensor_tensor_scan(dst, tile[:, k, :], dbx[:, q % DBX_RING, k, :],
                                                   0.0 if h == 0 else carry[:, n:n + 1],
                                                   ALU.mult, ALU.add).then_inc(scans, 1)
                    if p == 0 and (s > 0 or before):
                        if main or s == 0:
                            take_y(b, s - 1)
                    if main:
                        if h == 0 or p in DVE_PAIRS:
                            dve.wait_ge(scans, b * 2 * POINTS + 2 * q + 2)
                        if h == 0:
                            n = dc * NS + 2 * p
                            src = h_pool if p in POOL_PAIRS else tile
                            dve.tensor_copy(carry[:, n:n + 2], src[:, :, L - 1]).then_inc(carried, 1)
                        if p in DVE_PAIRS:
                            done = dve_products(q)
                            if counts(count := b * dve_products(POINTS - 1) + done - PROD_RING):
                                dve.wait_ge(prod_used, count)
                            dve.tensor_tensor(prod[:, (done - 1) % PROD_RING], tile, bc[:, p, 1], ALU.mult) \
                               .then_inc(prod_dve, 1)
                    if main and xi_of(q, XI_CONV) and (h == 0 or after):
                        m, xs = xi_of(q, XI_CONV)
                        i = proj_index(xs, "xi", m % 2)
                        c = b * CH * DC + DC * h + DC + m
                        dve.wait_ge(proj_taken, b * len(PROJ) + PROJ_FIRST + i + 1)
                        dve.wait_ge(halo_ready, c + 1)
                        convolve(1 - h, m, c)
                    for hh, use in ((1, before), (0, main)):
                        for i in range(2):
                            n = b * 4 + i - (2 if hh else 0)
                            dst = x1[:, hh, 2 * i:2 * i + 2, :]
                            if use and q == O_AT[hh][i] + STATS_LAG:
                                dve.wait_ge(o_ready, n + 1)
                                if i == 0:
                                    dve.wait_ge(xb_ready, b * 2 + (0 if hh else 1))
                                    if counts(count := b * 4 - 8 + 4 if hh else b * 4 - 4 + 2):
                                        dve.wait_ge(t_ready, count)
                                    if counts(count := b * 16 - 16 if hh else b * 16):
                                        dve.wait_ge(x1_stored[hh], count)
                                dve.tensor_tensor(dst, shared[:, :].rearrange("p (r c) -> p r c", c=DM),
                                                  x_res[:, 2 * i:2 * i + 2, :], ALU.add).then_inc(o_sum, 1)
                                norm_stats(o_sum, o_stat, o_mv, n, i, dst)
                            if use and q == O_AT[hh][i] + NORM_LAG:
                                normalise(o_rstd, o_norm, n, i, dst)
                    if before:
                        for c in range(CYCLES):
                            if q == cycle_at(c) + UPD_AT:
                                dve.wait_ge(cprod_ready, b * CYCLES - CYCLES + c + 1)
                                dve.tensor_tensor(oT[:, 0, :], oT[:, 0, :], big[:, 0, :], ALU.add)
                                dve.tensor_tensor(oT[:, 1, :], oT[:, 1, :], big[:, 1, :], ALU.subtract) \
                                   .then_inc(updated, 1)
                        for e in range(4):
                            dst = residual[:, 2 * e:2 * e + 2, :]
                            if q == E_AT[e] + STATS_LAG:
                                dve.wait_ge(e_ready, b * 4 - 4 + e + 1)
                                dve.wait_ge(re_in, b * 16)
                                dve.tensor_tensor(dst, shared[:, :].rearrange("p (r c) -> p r c", c=DM), dst,
                                                  ALU.add).then_inc(e_sum, 1)
                                norm_stats(e_sum, e_stat, e_mv, b * 4 - 4 + e, e % 2, dst)
                            if q == late(E_AT[e] + NORM_LAG):
                                normalise(e_rstd, e_norm, b * 4 - 4 + e, e % 2, dst)

            each_batch(dve, body)

        @block.gpsimd
        def _(pool):
            def fill_halo(h, m, c, taken):
                count = in_register(pool, taken)
                pool.wait_ge(v_in_sem, 16)
                pool.wait_ge(proj_taken, count)
                if h == 0:
                    pool.memset(pre[:, m % 2, 0:HALO], 0.0)
                    pool.tensor_copy(halo[:, m, :], pre[:, m % 2, L:L + HALO]).then_inc(halo_ready, 1)
                else:
                    count = in_register(pool, c - DC + 1)
                    pool.wait_ge(v_in_sem, 16)
                    pool.wait_ge(halo_ready, count)
                    pool.tensor_copy(pre[:, m % 2, 0:HALO], halo[:, m, :]).then_inc(halo_ready, 1)

            def make_u(h, dc, par, n):
                pool.wait_ge(log_ready, n + 1)
                pool.tensor_tensor(delta[:, par, :], delta[:, par, :], log_part[:, :], ALU.add).then_inc(delta_ready, 1)
                pool.wait_ge(delta_ready, n + 1)
                pool.tensor_tensor(u[:, par, :], delta[:, par, :], xi[:, h, dc, :], ALU.mult).then_inc(u_ready, 1)

            pool.memset(eps_col[:, :], EPS)
            pool.wait_ge(v_in_sem, 16)
            pool.tensor_tensor(conv_bias[:, :],
                               vs("w_conv").rearrange("p (m k) -> p m k", k=TAPS)[:, :, TAPS - 1],
                               vs("b_in")[:, 0:DC], ALU.mult).then_inc(pool_setup, 1)
            pool.tensor_tensor(coef[:, 3:4], v("range"), v("sign"), ALU.mult).then_inc(pool_setup, 1)
            pool.tensor_scalar(coef[:, 2:3], v("sign"), 0.1, 0.0, ALU.mult, ALU.add)
            pool.wait_ge(pool_setup, 2)
            pool.tensor_tensor(conv_bias[:, :], conv_bias[:, :], vs("b_conv"), ALU.add).then_inc(pool_setup, 1)
            pool.tensor_scalar(coef[:, 0:1], coef[:, 3:4], 0.3, 0.0, ALU.mult, ALU.add)
            pool.tensor_scalar(coef[:, 1:2], coef[:, 3:4], 0.7, 0.0, ALU.mult, ALU.add).then_inc(pool_setup, 1)
            pool.wait_ge(act_setup, 1)
            pool.tensor_scalar(neg_a[:, :], neg_a[:, :], -1.0, 0.0, ALU.mult, ALU.add).then_inc(pool_setup, 1)
            pool.wait_ge(pool_setup, 5)
            for m in range(DC):
                fill_halo(0, m, m, m + 1)
            pool.wait_ge(xi_ready, DC)
            make_u(0, 0, 0, 0)

            def body(b):
                main, before, after = kinds(b)
                for q in range(POINTS):
                    s, p = q // NP, q % NP
                    h, dc = s // DC, s % DC
                    if main:
                        if p == 0:
                            pool.wait_ge(u_ready, b * SLOTS + s + 1)
                        if dc == 0:
                            pool.wait_ge(bc_in[p], b * 32 + 16 * (h + 1))
                        if counts(count := b * 2 * POINTS + 2 * (q - DBX_RING) + 2):
                            pool.wait_ge(scans, count)
                        pool.tensor_tensor(dbx[:, q % DBX_RING], u[:, s % 2, :].unsqueeze(1).broadcast_to([P, 2, L]),
                                           bc[:, p, 0], ALU.mult).then_inc(dbx_ready, 1)
                        for pp in POOL_PAIRS:
                            if p == min(pp + 4, NP - 1):
                                if h == 0:
                                    pool.wait_ge(carried, b * DC * NP + dc * NP + pp + 1)
                                else:
                                    pool.wait_ge(scans, b * 2 * POINTS + 2 * (s * NP + pp) + 2)
                                pool.tensor_tensor(h_pool[:, :, :], h_pool[:, :, :], bc[:, pp, 1], ALU.mult) \
                                    .then_inc(prod_pool, 1)
                    if p == 4 and (s > 0 or before) and (main or s == 0):
                        pool.wait_ge(y_taken, b * SLOTS + s)
                        ended = isinstance(b, int) and b == BATCH
                        i = proj_index((s - 1) % SLOTS, "res", 0,
                                       PROJ_LAST if ended or s > 0 and not after else PROJ)
                        pool.wait_ge(proj_taken, b * len(PROJ) + PROJ_FIRST + i + 1 - (len(PROJ) if s == 0 else 0))
                        pool.tensor_tensor(yg[:, (s - 1) % DC, :], yg[:, (s - 1) % DC, :], s_res[:, (s - 1) % 2, :],
                                           ALU.mult).then_inc(gated, 1)
                    if main and p == 5 and (s < SLOTS - 1 or after):
                        n = (s + 1) % SLOTS
                        if n % DC == 0:
                            pool.wait_ge(xi_ready, b * CH * DC + DC * (h + 2))
                        make_u(n // DC, n % DC, n % 2, b * SLOTS + s + 1)
                    if main and xi_of(q, XI_HALO) and (h == 0 or after):
                        m, xs = xi_of(q, XI_HALO)
                        i = proj_index(xs, "xi", m % 2)
                        fill_halo(1 - h, m, b * CH * DC + DC * h + DC + m, b * len(PROJ) + PROJ_FIRST + i + 1)
                    if main and p == 1 and dc == 2:
                        pool.wait_ge(xr_in, b * 32 + 16 * (h + 1))
                        pool.tensor_tensor(x_res[:, :, :], x_res[:, :, :],
                                           b_out.unsqueeze(1).broadcast_to([P, 4, DM]), ALU.add).then_inc(xb_ready, 1)
                    if before:
                        if q == cycle_at(0) + MULT_AT:
                            count = in_register(pool, b * 3)
                            pool.wait_ge(v_in_sem, 16)
                            pool.wait_ge(g_actd, count)
                            pool.tensor_scalar(coef[:, 3:4], g_act[:, 2:3], coef[:, 1:2], coef[:, 2:3],
                                               ALU.mult, ALU.add).then_inc(alpha_ready, 1)
                            count = in_register(pool, b)
                            pool.wait_ge(v_in_sem, 16)
                            pool.wait_ge(alpha_ready, count)
                        for c in range(CYCLES):
                            if q == cycle_at(c) + MULT_AT:
                                n = b * CYCLES - CYCLES + c + 1
                                count = in_register(pool, n)
                                pool.wait_ge(v_in_sem, 16)
                                pool.wait_ge(f_tanh, count)
                                pool.tensor_scalar(mid[:, :], mid[:, :], coef[:, 0:1], coef[:, 3:4],
                                                   ALU.mult, ALU.add).then_inc(cs_ready, 1)
                                pool.wait_ge(cs_ready, n)
                                pool.tensor_tensor(big[:, 0, :], mid[:, :], oT[:, 1, :], ALU.mult)
                                pool.tensor_tensor(big[:, 1, :], mid[:, :], oT[:, 0, :], ALU.mult) \
                                    .then_inc(cprod_ready, 1)

            each_batch(pool, body)


def kernel(**inputs):
    import numpy as np
    import concourse.bacc as bacc
    from concourse.bass_utils import run_bass_kernel_spmd

    g = {n: np.ascontiguousarray(a) for n, a in inputs.items()}
    a = lambda n: g["L0_attn_" + n]
    f = lambda n: g["L0_ffn_" + n]

    def stacked(m):
        k, n = m.shape
        if k < P:
            return np.concatenate([m, np.zeros((P - k, n), np.float32)], 0)
        return m.reshape(k // P, P, n).transpose(1, 0, 2).reshape(P, -1)

    def column(vec):
        return stacked(vec.reshape(-1, 1))

    def everywhere(vec):
        return np.broadcast_to(vec.reshape(1, -1), (P, vec.size))

    weights = np.concatenate([
        stacked(a("W_in").T), stacked(a("W_x").T), stacked(a("W_out").T),
        stacked(f("cn_w1")), stacked(f("cn_w2")), stacked(f("cn_w3")),
        stacked(np.broadcast_to(f("cn_w4"), (64, P))),
        stacked(f("gc_w1")), stacked(f("gc_w2")), stacked(np.broadcast_to(f("gc_w3"), (64, P))),
    ], 1)
    sign = np.ones((P, 1), np.float32)
    sign[P // 2:] = -1.0
    vectors = np.concatenate([
        column(a("b_in")), column(a("b_conv")), stacked(a("W_conv").reshape(DI, TAPS)), column(a("b_x")[:DI]),
        column(a("D")), stacked(a("A_log")), column(a("b_x")[DI:]), column(f("cn_b1")), column(f("cn_b2")),
        column(f("cn_b3")), everywhere(f("cn_b4")), column(f("gc_b1")), column(f("gc_b2")),
        everywhere(f("gc_b3")), everywhere(f("adaptive_range")), sign, np.eye(P, dtype=np.float32),
        everywhere(a("b_out")),
    ], 1)
    x = a("x")
    arrays = {"in_x": x, "in_xT": np.ascontiguousarray(x.transpose(0, 2, 1)),
              "in_weights": np.ascontiguousarray(weights), "in_vectors": np.ascontiguousarray(vectors)}
    nc = bacc.Bacc("TRN2", target_bir_lowering=False, num_devices=1)
    args = [nc.dram_tensor(n, arr.shape, mybir.dt.from_np(arr.dtype), kind="ExternalInput").ap()
            for n, arr in arrays.items()]
    out = nc.dram_tensor("out_0", [BATCH, SEQ, DM], F32, kind="ExternalOutput").ap()
    build(nc, *args, out)
    r = run_bass_kernel_spmd(nc, [arrays], core_ids=[0])
    return r.results[0]["out_0"]
```

```python
from contextlib import ExitStack

import concourse.bass as bass
from concourse import mybir

ALU = mybir.AluOpType
ACT = mybir.ActivationFunctionType
F32 = mybir.dt.float32

P = 128
BATCH, SEQ, DM = 16, 1024, 256
DI, NS, TAPS = 512, 16, 4
L = 512
CH = SEQ // L
DC = DI // P
NP = NS // 2
SLOTS = CH * DC
POINTS = SLOTS * NP
HALO = TAPS - 1
EPS = 1e-5
LN_EXP = "natural_log_exp_and_others"

POOL_PAIRS = (3,)
DVE_PAIRS = tuple(p for p in range(NP) if p not in POOL_PAIRS)
DBX_RING = 4
PROD_RING = 2

W_COLS = {}
_at = 0
for _name, _n in (("in", 2 * 2 * DI), ("x", 4 * (DI + 2 * NS)), ("out", 4 * DM), ("w1", 2 * 256),
                  ("w2", 2 * 128), ("w3", 64), ("w4", P), ("g1", 2 * 128), ("g2", 64), ("g3", P)):
    W_COLS[_name] = (_at, _at + _n)
    _at += _n
W_TOTAL = _at
V_COLS = {}
_at = 0
for _name, _n in (("b_in", 8), ("b_conv", 4), ("w_conv", 16), ("b_x", 4), ("D", 4), ("A", 64),
                  ("b_bc", 1), ("b1", 2), ("b2", 1), ("b3", 1), ("b4", 1), ("gb1", 1), ("gb2", 1),
                  ("gb3", 1), ("range", 1), ("sign", 1), ("eye", P), ("b_out", DM)):
    V_COLS[_name] = (_at, _at + _n)
    _at += _n
V_TOTAL = _at

PROJ = []
for _h in range(CH):
    for _s, _kinds in enumerate((("delta", "res", "xi", "xi"), ("delta", "res", "xi", "xi"),
                                 ("delta", "res", "bc"), ("delta", "res"))):
        PROJ += [(DC * _h + _s, _k) for _k in _kinds]
PROJ_LAST = [t for t in PROJ if t[0] < DC or t[1] == "res" or t[1] == "delta" and t[0] < SLOTS - 1]
PROJ_FIRST = 6
PROJ_PAIR = {"delta": 0, "res": 2, "bc": 7}
XI_PAIRS = (3, 7)
BANKS = 3

CYCLES = 3
F_PER = 10
F_AT = (0, 1, 2, 3, 5, 6, 7, 7, 11, 12)
GELU_AT = (6, 9, 12)
TANH_AT = 15
MULT_AT = 16
UPD_AT = 16
G_AT = (4, 8, 11)
T_AT = (4, 4, 6, 7)
E_AT = (57, 58, 58, 59)
O_AT = {1: (0, 1), 0: (35, 37)}


COPY_LAG = 3
STATS_LAG = 2
RSTD_LAG = 4
NORM_LAG = 5
CYCLE_AT = (9, 25, 41)
SILU_AT = (4, 4, 5, 4, 5, 4, 5, 4)
DELTA_AT = 3
BC_AT = 9
OFF_LAG = 4
GATE_AT = 2
U_AT = 6
XB_AT = 14
XI_TAKEN = (6, 9)
XI_CONV = (7, 10)
XI_HALO = (7, 10)


def late(q):
    return min(q, POINTS - 1)


def xi_of(q, at):
    for s in range(SLOTS):
        for n in range(2):
            if s % DC < 2 and NP * s + at[n] == q:
                return 2 * (s % DC) + n, s
    return None


def cycle_at(c):
    return CYCLE_AT[c]


def task_list(main, coupling, after):
    tasks = []
    if main:
        projections = PROJ if after else PROJ_LAST
        for i, (s, kind) in enumerate(projections):
            at = XI_PAIRS[i - proj_index(s, "xi", 0, projections)] if kind == "xi" else PROJ_PAIR[kind]
            tasks.append((NP * s + at, "p", i))
        tasks += [(q, "o", n) for n, q in enumerate(O_AT[0])]
    if coupling:
        tasks += [(q, "t", n) for n, q in enumerate(T_AT)] + [(q, "e", n) for n, q in enumerate(E_AT)]
        tasks += [(q, "o", n - 2) for n, q in enumerate(O_AT[1])]
        tasks += [(cycle_at(c) + q, "f", F_PER * c + n) for c in range(CYCLES) for n, q in enumerate(F_AT)]
        tasks += [(cycle_at(0) + q, "g", n) for n, q in enumerate(G_AT)]
    return sorted(tasks, key=lambda t: (t[0], "pogfte".index(t[1]), t[2]))


def taken_at(q, kind, n):
    if kind == "p":
        s, what = PROJ[n]
        if what == "xi":
            return NP * s + XI_TAKEN[n - proj_index(s, "xi")]
        return NP * s + {"delta": DELTA_AT, "res": SILU_AT[s], "bc": BC_AT}[what]
    return q + (STATS_LAG if kind in ("o", "e") else COPY_LAG)


def assign_banks():
    free, banks = [0] * BANKS, {}
    for q, kind, n in task_list(True, True, True):
        k = free.index(min(free))
        free[k] = taken_at(q, kind, n)
        banks[kind, n] = k
    return banks


def dve_products(q):
    return len(DVE_PAIRS) * (q // NP) + sum(p in DVE_PAIRS for p in range(q % NP + 1))


def proj_index(s, kind, nth=0, tasks=PROJ):
    return [i for i, t in enumerate(tasks) if t == (s, kind)][nth]


BANK_OF = assign_banks()


def bank_of(kind, n, projections=PROJ):
    if kind == "p" and projections is not PROJ:
        s, what = projections[n]
        n = proj_index(s, what, n - proj_index(s, what, 0, projections))
    return BANK_OF[kind, n]


def counts(n):
    return not isinstance(n, int) or n > 0


def build(nc, x, xT, weights, vectors, out):
    x1_dram = nc.dram_tensor("x1_scratch", [BATCH, SEQ, DM], F32, kind="Internal").ap()
    bc_dram = nc.dram_tensor("bc_scratch", [CH, 2, NS, L], F32, kind="Internal").ap()

    with ExitStack() as ctx:
        def sb(name, shape):
            return ctx.enter_context(nc.sbuf_tensor(name, shape, F32))

        def psum(name, shape):
            return ctx.enter_context(nc.psum_tensor(name, shape, F32))

        def sem(name):
            return ctx.enter_context(nc.semaphore(name))

        w_all = sb("w_all", [P, W_TOTAL])
        v_all = sb("v_all", [P, V_TOTAL])
        x_feat = sb("x_feat", [P, CH, 2, L])
        x_res = sb("x_res", [P, 4, DM])
        pre = sb("pre", [P, 2, HALO + L])
        halo = sb("halo", [P, DC, HALO])
        xi = sb("xi", [P, CH, DC, L])
        s_res = sb("s_res", [P, 2, L])
        delta = sb("delta", [P, 2, L])
        log_part = sb("log_part", [P, L])
        u = sb("u", [P, 2, L])
        bc_rows = sb("bc_rows", [2 * NS, L])
        bc = sb("bc", [P, NP, 2, 2, L])
        dbx = sb("dbx", [P, DBX_RING, 2, L])
        h_pool = sb("h_pool", [P, 2, L])
        prod = sb("prod", [P, PROD_RING, 2, L])
        carry = sb("carry", [P, DC * NS])
        yg = sb("yg", [P, DC, L])
        x1 = sb("x1", [P, CH, 4, DM])
        stats = sb("stats", [P, 6, 2, 6])
        mean_var = sb("mean_var", [P, 6, 2, 2])
        log_var = sb("log_var", [P, 6, 2])
        r_std = sb("r_std", [P, 6, 2])
        eps_col = sb("eps_col", [P, 1])
        oT = sb("oT", [P, 2, SEQ])
        big = sb("big", [P, 2, SEQ])
        mid = sb("mid", [P, SEQ])
        sums = sb("sums", [P, 4])
        g_act = sb("g_act", [P, 3])
        neg_a = sb("neg_a", [P, DC * NS])
        conv_bias = sb("conv_bias", [P, DC])
        half_b4 = sb("half_b4", [P, 1])
        coef = sb("coef", [P, 4])

        def w(name, k, n, rows=P):
            a, _ = W_COLS[name]
            return w_all[0:rows, a:a + k * n].rearrange("p (k n) -> p k n", k=k)

        def v(name, c=0, rows=P):
            a, _ = V_COLS[name]
            return v_all[0:rows, a + c:a + c + 1]

        def vs(name):
            a, e = V_COLS[name]
            return v_all[:, a:e]

        w_in, w_x, w_out = w("in", 2, 2 * DI), w("x", 4, DI + 2 * NS), w("out", 4, DM)
        w1, w2, w3 = w("w1", 2, 256), w("w2", 2, 128), w("w3", 1, 64)
        w4 = w("w4", 1, P, 64)
        g1, g2, g3 = w("g1", 2, 128), w("g2", 1, 64), w("g3", 1, P, 64)
        eye, b_out = vs("eye"), vs("b_out")
        residual = big[:, :, :].rearrange("p m t -> p (m t)").rearrange("p (k c) -> p k c", c=DM)

        da = psum("da", [P, 2, 2, L])
        y_sum = psum("y_sum", [P, L])
        banks = psum("banks", [P, BANKS, L])

        w_in_sem = sem("in_weights_loaded")
        w_rest_sem = sem("other_weights_loaded")
        v_in_sem = sem("vectors_loaded")
        xf_in = [sem(f"x_feat_loaded{i}") for i in range(CH)]
        xr_in = sem("x_res_loaded")
        bc_in = [sem(f"bc_loaded{i}") for i in range(NP)]
        bc_stored = sem("bc_stored")
        x1_stored = [sem(f"x1_stored{i}") for i in range(CH)]
        re_in = sem("residual_loaded")
        out_done = sem("out_stored")
        act_setup = sem("act_setup")
        pool_setup = sem("pool_setup")
        proj_ready = sem("proj_ready")
        proj_taken = sem("proj_taken")
        sp_step = sem("softplus_step")
        log_ready = sem("log_ready")
        delta_ready = sem("delta_ready")
        u_ready = sem("u_ready")
        halo_ready = sem("halo_ready")
        conv_step = sem("conv_step")
        xi_ready = sem("xi_ready")
        da_ready = sem("da_ready")
        dbx_ready = sem("dbx_ready")
        scans = sem("scans_done")
        carried = sem("carried")
        prod_dve = sem("products_by_vector")
        prod_pool = sem("products_by_gpsimd")
        pool_sums = sem("product_sums_by_gpsimd")
        prod_used = sem("products_used")
        y_ready = sem("y_ready")
        y_taken = sem("y_taken")
        gated = sem("gated")
        xb_ready = sem("residual_with_bias")
        o_ready, o_sum, o_stat, o_mv, o_rstd, o_norm = (sem("o_" + n) for n in
                                                        ("ready", "sum", "stat", "mv", "rstd", "norm"))
        e_ready, e_sum, e_stat, e_mv, e_rstd, e_norm = (sem("e_" + n) for n in
                                                        ("ready", "sum", "stat", "mv", "rstd", "norm"))
        o_log, e_log = sem("o_log"), sem("e_log")
        t_ready, t_taken = sem("t_ready"), sem("t_taken")
        f_ready, f_taken, f_gelu, f_tanh = sem("f_ready"), sem("f_taken"), sem("f_gelu"), sem("f_tanh")
        g_ready, g_taken, g_actd = sem("g_ready"), sem("g_taken"), sem("g_activated")
        alpha_ready, cs_ready, cprod_ready, updated = (sem(n) for n in (
            "alpha_ready", "coupling_ready", "coupling_products", "updated"))

        TAKEN = {"t": (t_taken, 4, 0), "f": (f_taken, CYCLES * F_PER, 0), "g": (g_taken, 3, 0),
                 "o": (o_sum, 4, 1), "e": (e_sum, 4, 0)}

        block = ctx.enter_context(nc.Block(no_gpsimd_drain=True))

        def in_register(eng, n):
            return n if isinstance(n, int) else eng.to_reg(n)

        def each_batch(eng, body):
            body(0)
            body(1)
            with eng.Fori(2, BATCH - 1) as b:
                body(b)
            body(BATCH - 1)
            body(BATCH)

        def alone(b):
            return isinstance(b, int) and b == BATCH

        def token_parts(b):
            return (slice(0, L), slice(L, SEQ)) if alone(b) else (slice(0, SEQ),)

        def updates(b):
            return b * CYCLES - CYCLES

        def kinds(b):
            if not isinstance(b, int):
                return True, True, True
            return b < BATCH, b > 0, b < BATCH - 1

        @block.sync
        def _(sp):
            def load_x_feat(b, h):
                sp.dma_start(x_feat[:, h], xT[b].rearrange("(k p) t -> p k t", p=P)[:, :, h * L:(h + 1) * L]) \
                  .then_inc(xf_in[h], 16)

            def store_bc(h):
                sp.dma_start(bc_dram[h].rearrange("a n t -> (a n) t"), bc_rows[:, :]).then_inc(bc_stored, 16)

            def load_bc(h, p):
                sp.dma_start(bc[:, p], bc_dram[h, :, 2 * p:2 * p + 2, :].partition_broadcast(P)) \
                  .then_inc(bc_in[p], 16)

            sp.dma_start(v_all[:, :], vectors).then_inc(v_in_sem, 16)
            load_x_feat(0, 0)
            first = W_COLS["x"][0]
            sp.dma_start(w_all[:, 0:first], weights[:, 0:first]).then_inc(w_in_sem, 16)
            sp.dma_start(w_all[:, first:], weights[:, first:]).then_inc(w_rest_sem, 16)
            load_x_feat(0, 1)
            sp.wait_ge(proj_taken, 5)
            store_bc(0)
            sp.wait_ge(bc_stored, 16)
            for p in range(NP):
                load_bc(0, p)

            def body(b):
                main, before, after = kinds(b)
                for h in range(CH):
                    if main:
                        if counts(count := b * 4 + 2 * h):
                            count = in_register(sp, count)
                            sp.wait_ge(v_in_sem, 16)
                            sp.wait_ge(o_sum, count)
                        sp.dma_start(x_res[:, :, :], x[b, h * L:(h + 1) * L, :].rearrange("(k p) c -> p k c", p=P)) \
                          .then_inc(xr_in, 16)
                    if h == 0 and before:
                        count = in_register(sp, b * 4)
                        sp.wait_ge(v_in_sem, 16)
                        sp.wait_ge(o_norm, count)
                        sp.dma_start(x1_dram[b - 1, L:SEQ, :].rearrange("(k p) c -> p k c", p=P), x1[:, 1]) \
                          .then_inc(x1_stored[1], 16)
                    if h == 1 and main:
                        count = in_register(sp, b * 4 + 2)
                        sp.wait_ge(v_in_sem, 16)
                        sp.wait_ge(o_norm, count)
                        sp.dma_start(x1_dram[b, 0:L, :].rearrange("(k p) c -> p k c", p=P), x1[:, 0]) \
                          .then_inc(x1_stored[0], 16)
                    if h == 1 and before:
                        count = in_register(sp, b * 16)
                        sp.wait_ge(v_in_sem, 16)
                        sp.wait_ge(x1_stored[0], count)
                        count = in_register(sp, b * 16)
                        sp.wait_ge(v_in_sem, 16)
                        sp.wait_ge(x1_stored[1], count)
                        count = in_register(sp, updates(b) + (2 if alone(b) else 1) * CYCLES)
                        sp.wait_ge(v_in_sem, 16)
                        sp.wait_ge(updated, count)
                        sp.dma_start(residual, x1_dram[b - 1].rearrange("(k p) c -> p k c", p=P)) \
                          .then_inc(re_in, 16)
                    if main and (h == 0 or after):
                        nh = 1 - h
                        count = in_register(sp, b * len(PROJ) + PROJ_FIRST + proj_index(DC * h + 2, "bc") + 1)
                        sp.wait_ge(v_in_sem, 16)
                        sp.wait_ge(proj_taken, count)
                        store_bc(nh)
                        count = in_register(sp, b * 32 + 16 * (h + 2))
                        sp.wait_ge(v_in_sem, 16)
                        sp.wait_ge(bc_stored, count)
                        for p in range(NP):
                            q = (DC * h + DC - 1) * NP + p
                            count = in_register(sp, b * POINTS + q + 1)
                            sp.wait_ge(v_in_sem, 16)
                            sp.wait_ge(dbx_ready, count)
                            if p in POOL_PAIRS:
                                count = in_register(sp, b * SLOTS + DC * h + DC)
                                sp.wait_ge(v_in_sem, 16)
                                sp.wait_ge(prod_pool, count)
                            else:
                                count = in_register(sp, b * dve_products(POINTS - 1) + dve_products(q))
                                sp.wait_ge(v_in_sem, 16)
                                sp.wait_ge(prod_dve, count)
                            load_bc(nh, p)
                        if h == 0 and after or h == 1 and after:
                            count = in_register(sp, b * len(PROJ) + PROJ_FIRST + proj_index(DC * h + DC - 1, "res") + 1)
                            sp.wait_ge(v_in_sem, 16)
                            sp.wait_ge(proj_ready, count)
                            load_x_feat(b + 1, h)
                    if h == 1 and before:
                        for i in range(CH):
                            count = in_register(sp, b * 4 - 4 + 2 * i + 2)
                            sp.wait_ge(v_in_sem, 16)
                            sp.wait_ge(e_norm, count)
                            sp.dma_start(out[b - 1, i * L:(i + 1) * L, :].rearrange("(k p) c -> p k c", p=P),
                                         residual[:, 4 * i:4 * i + 4, :]).then_inc(out_done, 16)

            each_batch(sp, body)
            sp.wait_ge(out_done, BATCH * CH * 16)
            for i in range(CH):
                sp.wait_ge(x1_stored[i], BATCH * 16)
            sp.wait_ge(bc_stored, BATCH * CH * 16)

        @block.tensor
        def _(pe):
            def proj_in(bank, h, col):
                for k in range(2):
                    mm = pe.matmul(banks[:, bank, :], w_in[:, k, col:col + P], x_feat[:, h, k, :],
                                   start=k == 0, stop=k == 1)
                mm.then_inc(proj_ready, 1)

            def proj_x(bank, h, col, n):
                for k in range(4):
                    mm = pe.matmul(banks[0:n, bank, :], w_x[:, k, col:col + n], xi[:, h, k, :],
                                   start=k == 0, stop=k == 3)
                mm.then_inc(proj_ready, 1)

            pe.wait_ge(v_in_sem, 16)
            pe.wait_ge(w_in_sem, 16)
            pe.wait_ge(xf_in[0], 16)
            for m in range(DC):
                if counts(count := m - 1):
                    pe.wait_ge(proj_taken, count)
                proj_in(m % 2, 0, m * P)
            pe.wait_ge(w_rest_sem, 16)
            pe.wait_ge(proj_taken, 3)
            pe.wait_ge(xi_ready, DC)
            proj_x(0, 0, DI, 2 * NS)
            pe.wait_ge(proj_taken, 4)
            proj_x(1, 0, 0, P)

            def run_proj(b, bank, tasks, i):
                s, kind = tasks[i]
                h = s // DC
                if kind == "delta":
                    n = (s + 1) % SLOTS
                    if n % DC == 0:
                        pe.wait_ge(xi_ready, b * CH * DC + DC * (h + 2))
                    proj_x(bank, n // DC, (n % DC) * P, P)
                elif kind == "res":
                    proj_in(bank, h, DI + (s % DC) * P)
                elif kind == "xi":
                    m = 2 * (s % DC) + (i - proj_index(s, "xi", 0, tasks))
                    if m == 0:
                        pe.wait_ge(xf_in[1 - h], b * 16 + 16 * (1 + h))
                    proj_in(bank, 1 - h, m * P)
                else:
                    pe.wait_ge(xi_ready, b * CH * DC + DC * (h + 2))
                    proj_x(bank, 1 - h, DI, 2 * NS)

            def await_bank(b, user):
                if user is None:
                    pe.wait_ge(proj_taken, PROJ_FIRST)
                    return
                kind, n, lag = user
                if kind == "p":
                    pe.wait_ge(proj_taken, (b - lag) * len(PROJ) + PROJ_FIRST + n + 1)
                else:
                    taken, per, own = TAKEN[kind]
                    pe.wait_ge(taken, b * per + n + 1 - (0 if own else per) - lag * per)

            def run_shared(b, bank, kind, n):
                shared = banks[:, bank, :]
                if kind == "t":
                    half, m = n // 2, n % 2
                    pe.wait_ge(o_norm, b * 4 - 4 + 2 * half + 2)
                    for k in range(4):
                        mm = pe.transpose(shared[:, k * P:(k + 1) * P], x1[:, half, k, m * P:(m + 1) * P], eye)
                    mm.then_inc(t_ready, 1)
                elif kind == "o":
                    i = n % 2
                    h = 0 if n >= 0 else 1
                    pe.wait_ge(gated, b * SLOTS + (DC if h == 0 else 0))
                    for r in range(2):
                        tb = 2 * i + r
                        for k in range(4):
                            mm = pe.matmul(shared[:, r * DM:(r + 1) * DM], yg[:, k, tb * P:(tb + 1) * P],
                                           w_out[:, k, :], start=k == 0, stop=k == 3)
                    mm.then_inc(o_ready, 1)
                elif kind == "e":
                    half, i = n // 2, n % 2
                    pe.wait_ge(updated, updates(b) + (2 if alone(b) else 1) * CYCLES)
                    for r in range(2):
                        for m in range(2):
                            t0 = half * L + (2 * i + r) * P
                            mm = pe.transpose(shared[:, r * DM + m * P:r * DM + (m + 1) * P],
                                              oT[:, m, t0:t0 + P], eye)
                    mm.then_inc(e_ready, 1)
                elif kind == "g":
                    if n == 0:
                        pe.wait_ge(t_taken, b * 4)
                        for m in range(2):
                            for half in range(2):
                                mm = pe.matmul(shared[:, 0:1], g1[:, m, :], sums[:, 2 * m + half:2 * m + half + 1],
                                               start=m + half == 0, stop=m + half == 2)
                    elif n == 1:
                        pe.wait_ge(g_taken if alone(b) else g_actd, b * 3 - 3 + 1)
                        mm = pe.matmul(shared[0:64, 0:1], g2[:, 0, :], g_act[:, 0:1], start=True, stop=True)
                    else:
                        pe.wait_ge(g_taken if alone(b) else g_actd, b * 3 - 3 + 2)
                        mm = pe.matmul(shared[:, 0:1], g3[:, 0, :], g_act[0:64, 1:2], start=True, stop=True)
                    mm.then_inc(g_ready, 1)
                else:
                    c, n = n // F_PER, n % F_PER
                    if n < 4:
                        half, m = n // 2, n % 2
                        if c:
                            pe.wait_ge(updated, updates(b) + (2 * c - 1 + half if alone(b) else c))
                        elif m == 0:
                            pe.wait_ge(t_taken, b * 4 - 4 + 2 * half + 2)
                        for k in range(2):
                            mm = pe.matmul(shared[:, :], w1[:, k, m * P:(m + 1) * P],
                                           oT[:, k, half * L:(half + 1) * L], start=k == 0, stop=k == 1)
                    else:
                        stage, half = (n - 4) // 2, n % 2
                        if alone(b):
                            pe.wait_ge(f_taken, (updates(b) + c) * F_PER + (2 + 2 * half, 5 + half, 7 + half)[stage])
                        elif half == 0:
                            pe.wait_ge(f_gelu, b * 9 - 9 + 3 * c + stage + 1)
                        t = slice(half * L, (half + 1) * L)
                        if stage == 0:
                            for k in range(2):
                                mm = pe.matmul(shared[:, :], w2[:, k, :], big[:, k, t], start=k == 0, stop=k == 1)
                        elif stage == 1:
                            mm = pe.matmul(shared[0:64, :], w3[:, 0, :], mid[:, t], start=True, stop=True)
                        else:
                            mm = pe.matmul(shared[:, :], w4[:, 0, :], big[0:64, 0, t], start=True, stop=True)
                    mm.then_inc(f_ready, 1)

            def add_pair(b, s, src, first, last, done):
                for k in range(2):
                    mm = pe.matmul(y_sum[:, :], eye, src[:, k, :], start=first and k == 0, stop=last and k == 1)
                    if k == 1:
                        mm.then_inc(done, 1)

            def body(b):
                main, before, after = kinds(b)
                tasks = task_list(main, before, after)
                projections = PROJ if after else PROJ_LAST
                users = [None] * BANKS
                if not (isinstance(b, int) and b == 0):
                    first, ended = isinstance(b, int) and b == 1, isinstance(b, int) and b == BATCH
                    for _, kind, n in task_list(True, not first, not ended):
                        users[bank_of(kind, n, PROJ_LAST if ended else PROJ)] = (kind, n, 1)
                for q in range(POINTS):
                    s, p = q // NP, q % NP
                    h = s // DC
                    if main:
                        if p in DVE_PAIRS:
                            if p == DVE_PAIRS[0]:
                                if counts(count := b * SLOTS + s):
                                    pe.wait_ge(y_taken, count)
                            pe.wait_ge(prod_dve, b * dve_products(POINTS - 1) + dve_products(q))
                            add_pair(b, s, prod[:, (dve_products(q) - 1) % PROD_RING], p == DVE_PAIRS[0],
                                     p == NP - 1 and not POOL_PAIRS,
                                     y_ready if p == NP - 1 and not POOL_PAIRS else prod_used)
                        if p == NP - 1 and POOL_PAIRS:
                            pe.wait_ge(pool_sums, b * SLOTS + s + 1)
                            pe.matmul(y_sum[:, :], eye, h_pool[:, 0, :], start=False, stop=True).then_inc(y_ready, 1)
                    for tq, kind, n in tasks:
                        if tq == q:
                            bank = bank_of(kind, n, projections)
                            await_bank(b, users[bank])
                            users[bank] = (kind, n, 0)
                            if kind == "p":
                                run_proj(b, bank, projections, n)
                            else:
                                run_shared(b, bank, kind, n)

            each_batch(pe, body)

        @block.scalar
        def _(act):
            def take_xi(bank, h, m, c):
                if counts(count := c * 3 - 3):
                    act.wait_ge(conv_step, count)
                if counts(count := c - 1):
                    act.wait_ge(halo_ready, count)
                act.activation(xi[:, h, m, :], banks[:, bank, :], ACT.Identity,
                               bias=conv_bias[:, m:m + 1], scale=v("w_conv", m * TAPS + TAPS - 1))
                act.activation(pre[:, m % 2, HALO:], banks[:, bank, :], ACT.Identity,
                               bias=v("b_in", m), scale=1.0).then_inc(proj_taken, 1)

            def take_delta(bank, dc, par, n):
                if counts(count := n):
                    act.wait_ge(u_ready, count)
                act.activation(log_part[:, :], banks[:, bank, :], ACT.Abs, bias=v("b_x", dc), scale=1.0) \
                   .then_inc(sp_step, 1)
                act.activation(delta[:, par, :], banks[:, bank, :], ACT.Relu, bias=v("b_x", dc), scale=1.0) \
                   .then_inc(proj_taken, 1)
                act.wait_ge(sp_step, n * 2 + 1)
                act.activation(log_part[:, :], log_part[:, :], ACT.Exp, scale=-1.0).then_inc(sp_step, 1)
                act.wait_ge(sp_step, n * 2 + 2)
                act.activation(log_part[:, :], log_part[:, :], ACT.Ln, bias=1.0, scale=1.0).then_inc(log_ready, 1)

            def r_stds(mv, log_done, rs, n, i):
                act.wait_ge(mv, n + 1)
                act.activation(log_var[:, i, :], mean_var[:, i, :, 1], ACT.Ln, bias=eps_col[:, 0:1], scale=1.0) \
                   .then_inc(log_done, 1)
                act.wait_ge(log_done, n + 1)
                act.activation(r_std[:, i, :], log_var[:, i, :], ACT.Exp, scale=-0.5).then_inc(rs, 1)

            def signed_alpha(b):
                act.activation(g_act[:, 2:3], g_act[:, 2:3], ACT.Tanh, scale=0.5).then_inc(g_actd, 1)
                act.wait_ge(g_actd, b * 3 - (2 if alone(b) else 0))
                act.activation(coef[:, 3:4], g_act[:, 2:3], ACT.Identity, bias=coef[:, 2:3], scale=coef[:, 1:2]) \
                   .then_inc(alpha_ready, 1)
                act.wait_ge(alpha_ready, b)

            def signed_coupling(t):
                act.activation(mid[:, t], mid[:, t], ACT.Identity, bias=coef[:, 3:4], scale=coef[:, 0:1]) \
                   .then_inc(cs_ready, 1)

            act.wait_ge(v_in_sem, 16)
            nc.scalar.preload_act_table_set(LN_EXP)
            act.activation(neg_a[:, :], vs("A"), ACT.Exp).then_inc(act_setup, 1)
            act.wait_ge(pool_setup, 5)
            for m in range(DC):
                act.wait_ge(proj_ready, m + 1)
                if m >= 2:
                    act.wait_ge(conv_step, 3 * (m - 1))
                    act.wait_ge(halo_ready, m - 1)
                take_xi(m % 2, 0, m, 0)
            for m in range(DC):
                act.wait_ge(conv_step, 3 * m + 3)
                act.activation(xi[:, 0, m, :], xi[:, 0, m, :], ACT.Silu).then_inc(xi_ready, 1)
            nc.scalar.preload_act_table_set(LN_EXP)
            act.wait_ge(proj_ready, 5)
            act.activation(bc_rows[:, :], banks[0:2 * NS, 0, :], ACT.Identity,
                           bias=v("b_bc", 0, 2 * NS), scale=1.0).then_inc(proj_taken, 1)
            act.wait_ge(proj_ready, 6)
            take_delta(1, 0, 0, 0)

            def body(b):
                main, before, after = kinds(b)
                for q in range(POINTS):
                    s, p = q // NP, q % NP
                    h, dc = s // DC, s % DC
                    projections = PROJ if after else PROJ_LAST
                    if main:
                        if p == 0:
                            act.wait_ge(delta_ready, b * SLOTS + s + 1)
                        if counts(count := b * 2 * POINTS + 2 * q - 2):
                            act.wait_ge(scans, count)
                        if (p - 2) % NP in DVE_PAIRS:
                            if counts(count := b * dve_products(POINTS - 1) + dve_products(q - 2)):
                                act.wait_ge(prod_dve, count)
                        for k in range(2):
                            n = 2 * p + k
                            e = act.activation(da[:, q % 2, k, :], delta[:, s % 2, :], ACT.Exp,
                                               scale=neg_a[:, dc * NS + n:dc * NS + n + 1])
                        e.then_inc(da_ready, 1)
                    if main and p == DELTA_AT and (s < SLOTS - 1 or after):
                        i = proj_index(s, "delta", 0, projections)
                        act.wait_ge(proj_ready, b * len(PROJ) + PROJ_FIRST + i + 1)
                        n = (s + 1) % SLOTS
                        take_delta(bank_of("p", i, projections), n % DC, n % 2, b * SLOTS + s + 1)
                    if main and q % (DC * NP) == 2 * NP + BC_AT and (h == 0 or after):
                        i = proj_index(DC * h + 2, "bc")
                        act.wait_ge(proj_ready, b * len(PROJ) + PROJ_FIRST + i + 1)
                        act.wait_ge(bc_stored, b * 32 + 16 * (h + 1))
                        act.activation(bc_rows[:, :], banks[0:2 * NS, bank_of("p", i), :], ACT.Identity,
                                       bias=v("b_bc", 0, 2 * NS), scale=1.0).then_inc(proj_taken, 1)
                    for tq, kind, n in (task_list(main, before, after) if before else []):
                        if tq + COPY_LAG != q or kind in ("p", "o", "e"):
                            continue
                        shared = banks[:, bank_of(kind, n), :]
                        if kind == "t":
                            half, m = n // 2, n % 2
                            act.wait_ge(t_ready, b * 4 - 4 + n + 1)
                            if counts(count := b * 4 - 4):
                                act.wait_ge(e_ready, count)
                            act.activation(oT[:, m, half * L:(half + 1) * L], shared[:, :], ACT.Identity,
                                           accum_out=sums[:, 2 * m + half:2 * m + half + 1]).then_inc(t_taken, 1)
                        elif kind == "g":
                            rows = 64 if n == 1 else P
                            act.wait_ge(g_ready, b * 3 - 3 + n + 1)
                            direct = ACT.Gelu if alone(b) and n < 2 else ACT.Identity
                            act.activation(g_act[0:rows, n:n + 1], shared[0:rows, 0:1], direct,
                                           bias=v(("gb1", "gb2", "gb3")[n], 0, rows),
                                           scale=1.0 / SEQ if n == 0 else 1.0).then_inc(g_taken, 1)
                        else:
                            c, task = n // F_PER, n % F_PER
                            act.wait_ge(f_ready, (b * 3 - 3) * F_PER + n + 1)
                            if task < 4:
                                half, m = task // 2, task % 2
                                if task == 0 and c == 0:
                                    if counts(count := b * 32 - 32):
                                        act.wait_ge(out_done, count)
                                elif task == 0 or task == 2 and c and alone(b):
                                    act.wait_ge(updated, updates(b) + (2 * c - 1 + half if alone(b) else c))
                                dst, bias, rows = big[:, m, half * L:(half + 1) * L], v("b1", m), P
                            else:
                                stage, half = (task - 4) // 2, task % 2
                                t = slice(half * L, (half + 1) * L)
                                dst, bias, rows = ((mid[:, t], v("b2"), P), (big[0:64, 0, t], v("b3", 0, 64), 64),
                                                   (mid[:, t], v("b4"), P))[stage]
                            if not alone(b):
                                act.activation(dst, shared[0:rows, :], ACT.Identity, bias=bias, scale=1.0) \
                                   .then_inc(f_taken, 1)
                            elif task < 8:
                                act.activation(dst, shared[0:rows, :], ACT.Gelu, bias=bias, scale=1.0) \
                                   .then_inc(f_taken, 1)
                            else:
                                if c == 0 and task == 8:
                                    act.wait_ge(g_taken, b * 3)
                                    signed_alpha(b)
                                act.activation(dst, shared[0:rows, :], ACT.Tanh, bias=half_b4[:, 0:1], scale=0.5) \
                                   .then_inc(f_taken, 1)
                                act.wait_ge(f_taken, (updates(b) + c) * F_PER + 9 + half)
                                signed_coupling(t)
                    for hh, use in ((1, before), (0, main)):
                        for i in range(2):
                            if use and q == O_AT[hh][i] + RSTD_LAG:
                                r_stds(o_mv, o_log, o_rstd, b * 4 + i - (2 if hh else 0), i)
                    for e in range(4 if before else 0):
                        if q == late(E_AT[e] + RSTD_LAG):
                            if alone(b) and e == 0:
                                nc.scalar.preload_act_table_set(LN_EXP)
                            r_stds(e_mv, e_log, e_rstd, b * 4 - 4 + e, 2 + e)
                    switched = False
                    if main and p == SILU_AT[s]:
                        i = proj_index(s, "res", 0, projections)
                        act.wait_ge(proj_ready, b * len(PROJ) + PROJ_FIRST + i + 1)
                        if counts(count := b * SLOTS + s - 1):
                            act.wait_ge(gated, count)
                        act.activation(s_res[:, s % 2, :], banks[:, bank_of("p", i, projections), :], ACT.Silu,
                                       bias=v("b_in", DC + dc), scale=1.0).then_inc(proj_taken, 1)
                        if dc in (1, 2) and (h == 0 or after):
                            for m in (2 * dc - 2, 2 * dc - 1):
                                act.wait_ge(conv_step, b * 24 + 12 * h + 12 + 3 * m + 3)
                                act.activation(xi[:, 1 - h, m, :], xi[:, 1 - h, m, :], ACT.Silu) \
                                   .then_inc(xi_ready, 1)
                        switched = True
                    for c in range(CYCLES if before and main else 0):
                        at = q - cycle_at(c)
                        taken = (b * 3 - 3 + c) * F_PER
                        if at == GELU_AT[0]:
                            act.wait_ge(f_taken, taken + 4)
                            act.activation(big[:, :, :], big[:, :, :], ACT.Gelu).then_inc(f_gelu, 1)
                            switched = True
                        if at == GELU_AT[1]:
                            act.wait_ge(f_taken, taken + 6)
                            act.activation(mid[:, :], mid[:, :], ACT.Gelu).then_inc(f_gelu, 1)
                            switched = True
                        if at == GELU_AT[2]:
                            act.wait_ge(f_taken, taken + 8)
                            act.activation(big[0:64, 0, :], big[0:64, 0, :], ACT.Gelu).then_inc(f_gelu, 1)
                            switched = True
                        if c == 0 and at in GELU_AT[1:]:
                            n = GELU_AT.index(at) - 1
                            rows = 64 if n == 1 else P
                            act.wait_ge(g_taken, b * 3 - 3 + n + 1)
                            act.activation(g_act[0:rows, n:n + 1], g_act[0:rows, n:n + 1], ACT.Gelu) \
                               .then_inc(g_actd, 1)
                        if at == TANH_AT:
                            if c == 0:
                                act.wait_ge(g_taken, b * 3)
                                signed_alpha(b)
                            act.wait_ge(f_taken, taken + 10)
                            act.activation(mid[:, :], mid[:, :], ACT.Tanh, scale=0.5).then_inc(f_tanh, 1)
                            act.wait_ge(f_tanh, updates(b) + c + 1)
                            signed_coupling(slice(0, SEQ))
                            switched = True
                    if switched:
                        nc.scalar.preload_act_table_set(LN_EXP)
                    if main and xi_of(q, XI_TAKEN) and (h == 0 or after):
                        m, xs = xi_of(q, XI_TAKEN)
                        i = proj_index(xs, "xi", m % 2)
                        act.wait_ge(proj_ready, b * len(PROJ) + PROJ_FIRST + i + 1)
                        if m == 0:
                            if counts(count := b * SLOTS + DC * h):
                                act.wait_ge(y_taken, count)
                        take_xi(bank_of("p", i), 1 - h, m, b * CH * DC + DC * h + DC + m)

            each_batch(act, body)

        @block.vector
        def _(dve):
            def convolve(h, m, c):
                for k in range(HALO):
                    if k:
                        dve.wait_ge(conv_step, c * 3 + k)
                    dve.scalar_tensor_tensor(out=xi[:, h, m, :], in0=pre[:, m % 2, k:k + L],
                                             scalar=v("w_conv", m * TAPS + k), in1=xi[:, h, m, :],
                                             op0=ALU.mult, op1=ALU.add).then_inc(conv_step, 1)

            def norm_stats(sums_, st, mv, n, i, dst):
                dve.wait_ge(sums_, n + 1)
                for r in range(2):
                    ins = dve.bn_stats(stats[:, i, r, :], dst[:, r, :])
                ins.then_inc(st, 1)
                count = in_register(dve, n + 1)
                dve.wait_ge(v_in_sem, 16)
                dve.wait_ge(st, count)
                for r in range(2):
                    ins = dve.bn_aggr(mean_var[:, i, r, :], stats[:, i, r, :])
                ins.then_inc(mv, 1)

            def normalise(rs, done, n, i, dst):
                dve.wait_ge(rs, n + 1)
                for r in range(2):
                    ins = dve.tensor_scalar(dst[:, r, :], dst[:, r, :], mean_var[:, i, r, 0:1], r_std[:, i, r:r + 1],
                                            ALU.subtract, ALU.mult)
                ins.then_inc(done, 1)

            for m in range(DC):
                dve.wait_ge(proj_taken, m + 1)
                dve.wait_ge(halo_ready, m + 1)
                convolve(0, m, m)

            def take_y(b, s):
                h, dc = (s // DC) % CH, s % DC
                dve.wait_ge(y_ready, b * SLOTS + s + 1)
                if dc == 0:
                    if counts(count := b * 4 + 2 * h):
                        dve.wait_ge(o_ready, count)
                dve.scalar_tensor_tensor(out=yg[:, dc, :], in0=xi[:, h, dc, :], scalar=v("D", dc), in1=y_sum[:, :],
                                         op0=ALU.mult, op1=ALU.add).then_inc(y_taken, 1)

            def body(b):
                main, before, after = kinds(b)
                for q in range(POINTS):
                    s, p = q // NP, q % NP
                    h, dc = s // DC, s % DC
                    tile = da[:, q % 2]
                    if main:
                        dve.wait_ge(da_ready, b * POINTS + q + 1)
                        dve.wait_ge(dbx_ready, b * POINTS + q + 1)
                        if p in POOL_PAIRS:
                            if counts(count := b * SLOTS + s):
                                dve.wait_ge(y_ready, count)
                        for k in range(2):
                            n = dc * NS + 2 * p + k
                            if h == 1 and k == 0:
                                dve.wait_ge(carried, b * DC * NP + dc * NP + p + 1)
                            dst = h_pool[:, k, :] if p in POOL_PAIRS else tile[:, k, :]
                            dve.tensor_tensor_scan(dst, tile[:, k, :], dbx[:, q % DBX_RING, k, :],
                                                   0.0 if h == 0 else carry[:, n:n + 1],
                                                   ALU.mult, ALU.add).then_inc(scans, 1)
                    if p == 0 and (s > 0 or before):
                        if main or s == 0:
                            take_y(b, s - 1)
                    if main:
                        if h == 0 or p in DVE_PAIRS:
                            dve.wait_ge(scans, b * 2 * POINTS + 2 * q + 2)
                        if h == 0:
                            n = dc * NS + 2 * p
                            src = h_pool if p in POOL_PAIRS else tile
                            dve.tensor_copy(carry[:, n:n + 2], src[:, :, L - 1]).then_inc(carried, 1)
                        if p in DVE_PAIRS:
                            done = dve_products(q)
                            if counts(count := b * dve_products(POINTS - 1) + done - PROD_RING):
                                dve.wait_ge(prod_used, count)
                            dve.tensor_tensor(prod[:, (done - 1) % PROD_RING], tile, bc[:, p, 1], ALU.mult) \
                               .then_inc(prod_dve, 1)
                    if main and xi_of(q, XI_CONV) and (h == 0 or after):
                        m, xs = xi_of(q, XI_CONV)
                        i = proj_index(xs, "xi", m % 2)
                        c = b * CH * DC + DC * h + DC + m
                        dve.wait_ge(proj_taken, b * len(PROJ) + PROJ_FIRST + i + 1)
                        dve.wait_ge(halo_ready, c + 1)
                        convolve(1 - h, m, c)
                    for hh, use in ((1, before), (0, main)):
                        for i in range(2):
                            n = b * 4 + i - (2 if hh else 0)
                            dst = x1[:, hh, 2 * i:2 * i + 2, :]
                            if use and q == O_AT[hh][i] + STATS_LAG:
                                dve.wait_ge(o_ready, n + 1)
                                if i == 0:
                                    dve.wait_ge(xb_ready, b * 2 + (0 if hh else 1))
                                    if counts(count := b * 4 - 8 + 4 if hh else b * 4 - 4 + 2):
                                        dve.wait_ge(t_ready, count)
                                    if counts(count := b * 16 - 16 if hh else b * 16):
                                        dve.wait_ge(x1_stored[hh], count)
                                shared = banks[:, bank_of("o", i - 2 * hh), :]
                                dve.tensor_tensor(dst, shared.rearrange("p (r c) -> p r c", c=DM),
                                                  x_res[:, 2 * i:2 * i + 2, :], ALU.add).then_inc(o_sum, 1)
                                norm_stats(o_sum, o_stat, o_mv, n, i, dst)
                            if use and q == O_AT[hh][i] + NORM_LAG:
                                normalise(o_rstd, o_norm, n, i, dst)
                    if before:
                        for c in range(CYCLES):
                            if q == cycle_at(c) + UPD_AT:
                                for i, t in enumerate(token_parts(b)):
                                    dve.wait_ge(cprod_ready, updates(b) + (2 * c + i if alone(b) else c) + 1)
                                    dve.tensor_tensor(oT[:, 0, t], oT[:, 0, t], big[:, 0, t], ALU.add)
                                    dve.tensor_tensor(oT[:, 1, t], oT[:, 1, t], big[:, 1, t], ALU.subtract) \
                                       .then_inc(updated, 1)
                        for e in range(4):
                            dst = residual[:, 2 * e:2 * e + 2, :]
                            if q == E_AT[e] + STATS_LAG:
                                dve.wait_ge(e_ready, b * 4 - 4 + e + 1)
                                dve.wait_ge(re_in, b * 16)
                                shared = banks[:, bank_of("e", e), :]
                                dve.tensor_tensor(dst, shared.rearrange("p (r c) -> p r c", c=DM), dst,
                                                  ALU.add).then_inc(e_sum, 1)
                                norm_stats(e_sum, e_stat, e_mv, b * 4 - 4 + e, 2 + e, dst)
                            if q == late(E_AT[e] + NORM_LAG):
                                normalise(e_rstd, e_norm, b * 4 - 4 + e, 2 + e, dst)

            each_batch(dve, body)

        @block.gpsimd
        def _(pool):
            def fill_halo(h, m, c, taken):
                count = in_register(pool, taken)
                pool.wait_ge(v_in_sem, 16)
                pool.wait_ge(proj_taken, count)
                if h == 0:
                    pool.memset(pre[:, m % 2, 0:HALO], 0.0)
                    pool.tensor_copy(halo[:, m, :], pre[:, m % 2, L:L + HALO]).then_inc(halo_ready, 1)
                else:
                    count = in_register(pool, c - DC + 1)
                    pool.wait_ge(v_in_sem, 16)
                    pool.wait_ge(halo_ready, count)
                    pool.tensor_copy(pre[:, m % 2, 0:HALO], halo[:, m, :]).then_inc(halo_ready, 1)

            def make_u(h, dc, par, n):
                pool.wait_ge(log_ready, n + 1)
                pool.tensor_tensor(delta[:, par, :], delta[:, par, :], log_part[:, :], ALU.add).then_inc(delta_ready, 1)
                pool.wait_ge(delta_ready, n + 1)
                pool.tensor_tensor(u[:, par, :], delta[:, par, :], xi[:, h, dc, :], ALU.mult).then_inc(u_ready, 1)

            pool.memset(eps_col[:, :], EPS)
            pool.wait_ge(v_in_sem, 16)
            pool.tensor_tensor(conv_bias[:, :],
                               vs("w_conv").rearrange("p (m k) -> p m k", k=TAPS)[:, :, TAPS - 1],
                               vs("b_in")[:, 0:DC], ALU.mult).then_inc(pool_setup, 1)
            pool.tensor_tensor(coef[:, 3:4], v("range"), v("sign"), ALU.mult).then_inc(pool_setup, 1)
            pool.tensor_scalar(coef[:, 2:3], v("sign"), 0.1, 0.0, ALU.mult, ALU.add)
            pool.tensor_scalar(half_b4[:, 0:1], v("b4"), 0.5, 0.0, ALU.mult, ALU.add)
            pool.wait_ge(pool_setup, 2)
            pool.tensor_tensor(conv_bias[:, :], conv_bias[:, :], vs("b_conv"), ALU.add).then_inc(pool_setup, 1)
            pool.tensor_scalar(coef[:, 0:1], coef[:, 3:4], 0.3, 0.0, ALU.mult, ALU.add)
            pool.tensor_scalar(coef[:, 1:2], coef[:, 3:4], 0.7, 0.0, ALU.mult, ALU.add).then_inc(pool_setup, 1)
            pool.wait_ge(act_setup, 1)
            pool.tensor_scalar(neg_a[:, :], neg_a[:, :], -1.0, 0.0, ALU.mult, ALU.add).then_inc(pool_setup, 1)
            pool.wait_ge(pool_setup, 5)
            for m in range(DC):
                fill_halo(0, m, m, m + 1)
            pool.wait_ge(xi_ready, DC)
            make_u(0, 0, 0, 0)

            def body(b):
                main, before, after = kinds(b)
                for q in range(POINTS):
                    s, p = q // NP, q % NP
                    h, dc = s // DC, s % DC
                    if main:
                        if p == 0:
                            pool.wait_ge(u_ready, b * SLOTS + s + 1)
                        if dc == 0:
                            pool.wait_ge(bc_in[p], b * 32 + 16 * (h + 1))
                        if counts(count := b * 2 * POINTS + 2 * (q - DBX_RING) + 2):
                            pool.wait_ge(scans, count)
                        pool.tensor_tensor(dbx[:, q % DBX_RING], u[:, s % 2, :].unsqueeze(1).broadcast_to([P, 2, L]),
                                           bc[:, p, 0], ALU.mult).then_inc(dbx_ready, 1)
                        for pp in POOL_PAIRS:
                            if p == min(pp + OFF_LAG, NP - 1):
                                if h == 0:
                                    pool.wait_ge(carried, b * DC * NP + dc * NP + pp + 1)
                                else:
                                    pool.wait_ge(scans, b * 2 * POINTS + 2 * (s * NP + pp) + 2)
                                pool.tensor_tensor(h_pool[:, :, :], h_pool[:, :, :], bc[:, pp, 1], ALU.mult) \
                                    .then_inc(prod_pool, 1)
                                pool.wait_ge(prod_pool, b * SLOTS + s + 1)
                                pool.tensor_tensor(h_pool[:, 0, :], h_pool[:, 0, :], h_pool[:, 1, :], ALU.add) \
                                    .then_inc(pool_sums, 1)
                    if p == GATE_AT and (s > 0 or before) and (main or s == 0):
                        pool.wait_ge(y_taken, b * SLOTS + s)
                        ended = isinstance(b, int) and b == BATCH
                        i = proj_index((s - 1) % SLOTS, "res", 0,
                                       PROJ_LAST if ended or s > 0 and not after else PROJ)
                        pool.wait_ge(proj_taken, b * len(PROJ) + PROJ_FIRST + i + 1 - (len(PROJ) if s == 0 else 0))
                        pool.tensor_tensor(yg[:, (s - 1) % DC, :], yg[:, (s - 1) % DC, :], s_res[:, (s - 1) % 2, :],
                                           ALU.mult).then_inc(gated, 1)
                    if main and p == U_AT and (s < SLOTS - 1 or after):
                        n = (s + 1) % SLOTS
                        if n % DC == 0:
                            pool.wait_ge(xi_ready, b * CH * DC + DC * (h + 2))
                        make_u(n // DC, n % DC, n % 2, b * SLOTS + s + 1)
                    if main and xi_of(q, XI_HALO) and (h == 0 or after):
                        m, xs = xi_of(q, XI_HALO)
                        i = proj_index(xs, "xi", m % 2)
                        fill_halo(1 - h, m, b * CH * DC + DC * h + DC + m, b * len(PROJ) + PROJ_FIRST + i + 1)
                    if main and q % (DC * NP) == XB_AT:
                        pool.wait_ge(xr_in, b * 32 + 16 * (h + 1))
                        pool.tensor_tensor(x_res[:, :, :], x_res[:, :, :],
                                           b_out.unsqueeze(1).broadcast_to([P, 4, DM]), ALU.add).then_inc(xb_ready, 1)
                    if before:
                        for c in range(CYCLES):
                            if q == cycle_at(c) + MULT_AT:
                                for i, t in enumerate(token_parts(b)):
                                    n = updates(b) + (2 * c + i if alone(b) else c) + 1
                                    pool.wait_ge(cs_ready, n)
                                    pool.tensor_tensor(big[:, 0, t], mid[:, t], oT[:, 1, t], ALU.mult)
                                    pool.tensor_tensor(big[:, 1, t], mid[:, t], oT[:, 0, t], ALU.mult) \
                                        .then_inc(cprod_ready, 1)

            each_batch(pool, body)


def kernel(**inputs):
    import numpy as np
    import concourse.bacc as bacc
    from concourse.bass_utils import run_bass_kernel_spmd

    g = {n: np.ascontiguousarray(a) for n, a in inputs.items()}
    a = lambda n: g["L0_attn_" + n]
    f = lambda n: g["L0_ffn_" + n]

    def stacked(m):
        k, n = m.shape
        if k < P:
            return np.concatenate([m, np.zeros((P - k, n), np.float32)], 0)
        return m.reshape(k // P, P, n).transpose(1, 0, 2).reshape(P, -1)

    def column(vec):
        return stacked(vec.reshape(-1, 1))

    def everywhere(vec):
        return np.broadcast_to(vec.reshape(1, -1), (P, vec.size))

    weights = np.concatenate([
        stacked(a("W_in").T), stacked(a("W_x").T), stacked(a("W_out").T),
        stacked(f("cn_w1")), stacked(f("cn_w2")), stacked(f("cn_w3")),
        stacked(np.broadcast_to(f("cn_w4"), (64, P))),
        stacked(f("gc_w1")), stacked(f("gc_w2")), stacked(np.broadcast_to(f("gc_w3"), (64, P))),
    ], 1)
    sign = np.ones((P, 1), np.float32)
    sign[P // 2:] = -1.0
    vectors = np.concatenate([
        column(a("b_in")), column(a("b_conv")), stacked(a("W_conv").reshape(DI, TAPS)), column(a("b_x")[:DI]),
        column(a("D")), stacked(a("A_log")), column(a("b_x")[DI:]), column(f("cn_b1")), column(f("cn_b2")),
        column(f("cn_b3")), everywhere(f("cn_b4")), column(f("gc_b1")), column(f("gc_b2")),
        everywhere(f("gc_b3")), everywhere(f("adaptive_range")), sign, np.eye(P, dtype=np.float32),
        everywhere(a("b_out")),
    ], 1)
    x = a("x")
    arrays = {"in_x": x, "in_xT": np.ascontiguousarray(x.transpose(0, 2, 1)),
              "in_weights": np.ascontiguousarray(weights), "in_vectors": np.ascontiguousarray(vectors)}
    nc = bacc.Bacc("TRN2", target_bir_lowering=False, num_devices=1)
    args = [nc.dram_tensor(n, arr.shape, mybir.dt.from_np(arr.dtype), kind="ExternalInput").ap()
            for n, arr in arrays.items()]
    out = nc.dram_tensor("out_0", [BATCH, SEQ, DM], F32, kind="ExternalOutput").ap()
    build(nc, *args, out)
    r = run_bass_kernel_spmd(nc, [arrays], core_ids=[0])
    return r.results[0]["out_0"]
```
